# Optimizing a Trainium2 kernel written in Bass

```python
import numpy as np
import jax
import jax.numpy as jnp

def _softmax(x, axis=-1):
    return jax.nn.softmax(x, axis=axis)

def _gelu(x):
    return jax.nn.gelu(x, approximate=True)

def _silu(x):
    return jax.nn.silu(x)

def _sigmoid(x):
    return jax.nn.sigmoid(x)

def _layernorm(x, axis=-1, eps=1e-05):
    m = jnp.mean(x, axis=axis, keepdims=True)
    v = jnp.var(x, axis=axis, keepdims=True)
    return (x - m) / jnp.sqrt(v + eps)

def _scatter_add(tgt, idx, src, axis=0):
    return tgt.at[idx].add(src)

def _segment_sum(src, seg, n):
    return jax.ops.segment_sum(src, seg, n)
kernel_name = 'mk_gnn_preln_d4_gnn_r64_153d70'

def setup_inputs(seed: int=0):
    np.random.seed(seed)
    _w = jnp.asarray

    def _rec_inputs():
        import jax
        import jax.numpy as jnp
        _gk = jax.random.key(seed)
        x = -0.000202 + 1 * jax.random.normal(jax.random.fold_in(_gk, 1), (50000, 128), jnp.float32)
        src = jax.random.randint(jax.random.fold_in(_gk, 2), (12500,), 0, 50000, jnp.int32)
        dst = jnp.minimum((50000 * jax.random.uniform(jax.random.fold_in(_gk, 3), (12500,)) ** 2.0).astype(jnp.int32), 49999)
        _o = jnp.argsort(dst, stable=True)
        src = src[_o]
        dst = dst[_o]
        edge_attr_128 = -8.513e-05 + 0.999844 * jax.random.normal(jax.random.fold_in(_gk, 12), (12500, 128), jnp.float32)
        edge_weight = jax.random.uniform(jax.random.fold_in(_gk, 14), (12500,), jnp.float32, 0.0, 0.999998)
        return (x, src, dst, edge_attr_128, edge_weight)
    x, src, dst, edge_attr_128, edge_weight = _rec_inputs()

    def _L0_gnn_setup():
        import jax, jax.numpy as jnp
        import numpy as np
        N_NODES = 50000
        N_EDGES = 12500
        D = 128

        def _gcn_norm(edge_index, edge_weights, n_nodes):
            src = jnp.concatenate([edge_index[0], jnp.arange(n_nodes)])
            dst = jnp.concatenate([edge_index[1], jnp.arange(n_nodes)])
            w = jnp.concatenate([edge_weights, jnp.ones((n_nodes,), edge_weights.dtype)])
            deg = jax.ops.segment_sum(w, dst, num_segments=n_nodes)
            dinv = jnp.where(deg > 0, jax.lax.rsqrt(deg), 0.0)
            norm = dinv[src] * w * dinv[dst]
            return (src, dst, norm)

        def _gcn_conv(x, src, dst, norm, W, b, n_nodes):
            h = x @ W
            msg = h[src] * norm[:, None]
            out = jax.ops.segment_sum(msg, dst, num_segments=n_nodes)
            return out + b
        key = jax.random.key(seed)
        ks = jax.random.split(key, 12)
        s = 1.0 / np.sqrt(D)
        return {'x': jax.random.normal(ks[0], (N_NODES, D), jnp.float32), 'edge_index': jax.random.randint(ks[1], (2, N_EDGES), 0, N_NODES, jnp.int64), 'edge_weights': jax.random.uniform(ks[2], (N_EDGES,), jnp.float32), 'W1': jax.random.normal(ks[3], (D, D), jnp.float32) * s, 'b1': jnp.zeros((D,), jnp.float32), 'W2': jax.random.normal(ks[4], (D, D), jnp.float32) * s, 'b2': jnp.zeros((D,), jnp.float32), 'W3': jax.random.normal(ks[5], (D, D), jnp.float32) * s, 'b3': jnp.zeros((D,), jnp.float32), 'Wl': jax.random.normal(ks[6], (D, D), jnp.float32) * s, 'bl': jnp.zeros((D,), jnp.float32)}
    _L0_gnn_all = _L0_gnn_setup()
    _L0_gnn_in = {k: v for k, v in _L0_gnn_all.items() if k in ('W1', 'b1', 'W2', 'b2', 'W3', 'b3', 'Wl', 'bl')}
    del _L0_gnn_all

    def _L1_gnn_setup():
        import jax, jax.numpy as jnp
        import numpy as np
        N_NODES = 10000
        N_EDGES = 10000
        D = 128
        BN_EPS = 1e-05

        def _batchnorm(x, gamma, beta):
            mu = jnp.mean(x, axis=0)
            var = jnp.mean(jnp.square(x - mu), axis=0)
            return (x - mu) * jax.lax.rsqrt(var + BN_EPS) * gamma + beta
        key = jax.random.key(seed)
        ks = jax.random.split(key, 8)
        node_feats = jax.random.normal(ks[0], (N_NODES, D), dtype=jnp.float32)
        edge_feats = jax.random.normal(ks[1], (N_EDGES, D), dtype=jnp.float32)
        src = jax.random.randint(ks[2], (N_EDGES,), 0, N_NODES)
        dst = jax.random.randint(ks[3], (N_EDGES,), 0, N_NODES)
        W1 = jax.random.normal(ks[4], (D, 2 * D), dtype=jnp.float32) * (1.0 / np.sqrt(D))
        b1 = jnp.zeros((2 * D,), dtype=jnp.float32)
        gamma1 = jnp.ones((2 * D,), dtype=jnp.float32)
        beta1 = jnp.zeros((2 * D,), dtype=jnp.float32)
        W2 = jax.random.normal(ks[5], (2 * D, D), dtype=jnp.float32) * (1.0 / np.sqrt(2 * D))
        b2 = jnp.zeros((D,), dtype=jnp.float32)
        gamma2 = jnp.ones((D,), dtype=jnp.float32)
        beta2 = jnp.zeros((D,), dtype=jnp.float32)
        eps = jnp.zeros((1,), dtype=jnp.float32)
        return {'node_feats': node_feats, 'edge_feats': edge_feats, 'eps': eps, 'W1': W1, 'b1': b1, 'gamma1': gamma1, 'beta1': beta1, 'W2': W2, 'b2': b2, 'gamma2': gamma2, 'beta2': beta2, 'src': src, 'dst': dst}
    _L1_gnn_all = _L1_gnn_setup()
    _L1_gnn_in = {k: v for k, v in _L1_gnn_all.items() if k in ('eps', 'W1', 'b1', 'gamma1', 'beta1', 'W2', 'b2', 'gamma2', 'beta2')}
    del _L1_gnn_all

    def _L2_gnn_setup():
        import jax, jax.numpy as jnp
        import numpy as np
        N_NODES = 100000
        N_EDGES = 25000
        HIDDEN = 128
        DEPTH = 6
        key = jax.random.key(seed)
        k1, k2, k3, k4 = jax.random.split(key, 4)
        x = jax.random.normal(k1, (N_NODES, HIDDEN), dtype=jnp.float32)
        edge_index = jax.random.randint(k2, (2, N_EDGES), 0, N_NODES, dtype=jnp.int64)
        W_h_weight = jax.random.normal(k3, (HIDDEN, HIDDEN), dtype=jnp.float32) * (1.0 / np.sqrt(HIDDEN))
        W_h_bias = jax.random.normal(k4, (HIDDEN,), dtype=jnp.float32) * (1.0 / np.sqrt(HIDDEN))
        return {'x': x, 'edge_index': edge_index, 'W_h_weight': W_h_weight, 'W_h_bias': W_h_bias}
    _L2_gnn_all = _L2_gnn_setup()
    _L2_gnn_in = {k: v for k, v in _L2_gnn_all.items() if k in ('W_h_weight', 'W_h_bias')}
    del _L2_gnn_all

    def _L3_gnn_setup():
        import jax, jax.numpy as jnp
        import numpy as np
        N_NODES = 50000
        N_EDGES = 10000
        D_IN = 128
        D_HID = 128
        D_OUT = 128

        def gcn_conv(x, edge_index, W, b, num_nodes):
            loops = jnp.arange(num_nodes, dtype=edge_index.dtype)
            src = jnp.concatenate([edge_index[0], loops])
            dst = jnp.concatenate([edge_index[1], loops])
            deg = jax.ops.segment_sum(jnp.ones_like(dst, dtype=x.dtype), dst, num_segments=num_nodes)
            dinv = jnp.where(deg > 0, jax.lax.rsqrt(deg), 0.0)
            norm = dinv[src] * dinv[dst]
            h = x @ W
            msg = norm[:, None] * h[src]
            out = jax.ops.segment_sum(msg, dst, num_segments=num_nodes)
            return out + b
        key = jax.random.key(seed)
        k1, k2, k3, k4 = jax.random.split(key, 4)
        x = jax.random.normal(k1, (N_NODES, D_IN), dtype=jnp.float32)
        edge_index = jax.random.randint(k2, (2, N_EDGES), 0, N_NODES, dtype=jnp.int32)
        W1 = jax.random.normal(k3, (D_IN, D_HID), dtype=jnp.float32) * (1.0 / np.sqrt(D_IN))
        b1 = jnp.zeros((D_HID,), dtype=jnp.float32)
        W2 = jax.random.normal(k4, (D_HID, D_OUT), dtype=jnp.float32) * (1.0 / np.sqrt(D_HID))
        b2 = jnp.zeros((D_OUT,), dtype=jnp.float32)
        return {'x': x, 'edge_index': edge_index, 'W1': W1, 'b1': b1, 'W2': W2, 'b2': b2}
    _L3_gnn_all = _L3_gnn_setup()
    _L3_gnn_in = {k: v for k, v in _L3_gnn_all.items() if k in ('W1', 'b1', 'W2', 'b2')}
    del _L3_gnn_all
    return {'x': x, 'src': src, 'dst': dst, 'edge_attr_128': edge_attr_128, 'edge_weight': edge_weight, 'L0_gnn_W1': _L0_gnn_in['W1'], 'L0_gnn_b1': _L0_gnn_in['b1'], 'L0_gnn_W2': _L0_gnn_in['W2'], 'L0_gnn_b2': _L0_gnn_in['b2'], 'L0_gnn_W3': _L0_gnn_in['W3'], 'L0_gnn_b3': _L0_gnn_in['b3'], 'L0_gnn_Wl': _L0_gnn_in['Wl'], 'L0_gnn_bl': _L0_gnn_in['bl'], 'L1_gnn_eps': _L1_gnn_in['eps'], 'L1_gnn_W1': _L1_gnn_in['W1'], 'L1_gnn_b1': _L1_gnn_in['b1'], 'L1_gnn_gamma1': _L1_gnn_in['gamma1'], 'L1_gnn_beta1': _L1_gnn_in['beta1'], 'L1_gnn_W2': _L1_gnn_in['W2'], 'L1_gnn_b2': _L1_gnn_in['b2'], 'L1_gnn_gamma2': _L1_gnn_in['gamma2'], 'L1_gnn_beta2': _L1_gnn_in['beta2'], 'L2_gnn_W_h_weight': _L2_gnn_in['W_h_weight'], 'L2_gnn_W_h_bias': _L2_gnn_in['W_h_bias'], 'L3_gnn_W1': _L3_gnn_in['W1'], 'L3_gnn_b1': _L3_gnn_in['b1'], 'L3_gnn_W2': _L3_gnn_in['W2'], 'L3_gnn_b2': _L3_gnn_in['b2']}

def reference(x, src, dst, edge_attr_128, edge_weight, L0_gnn_W1, L0_gnn_b1, L0_gnn_W2, L0_gnn_b2, L0_gnn_W3, L0_gnn_b3, L0_gnn_Wl, L0_gnn_bl, L1_gnn_eps, L1_gnn_W1, L1_gnn_b1, L1_gnn_gamma1, L1_gnn_beta1, L1_gnn_W2, L1_gnn_b2, L1_gnn_gamma2, L1_gnn_beta2, L2_gnn_W_h_weight, L2_gnn_W_h_bias, L3_gnn_W1, L3_gnn_b1, L3_gnn_W2, L3_gnn_b2):
    import jax
    import jax.numpy as jnp

    def _L0_gnn_ref(x, edge_index, edge_weights, W1, b1, W2, b2, W3, b3, Wl, bl):
        import jax, jax.numpy as jnp
        import numpy as np
        N_NODES = 50000
        N_EDGES = 12500
        D = 128

        def _gcn_norm(edge_index, edge_weights, n_nodes):
            src = jnp.concatenate([edge_index[0], jnp.arange(n_nodes)])
            dst = jnp.concatenate([edge_index[1], jnp.arange(n_nodes)])
            w = jnp.concatenate([edge_weights, jnp.ones((n_nodes,), edge_weights.dtype)])
            deg = jax.ops.segment_sum(w, dst, num_segments=n_nodes)
            dinv = jnp.where(deg > 0, jax.lax.rsqrt(deg), 0.0)
            norm = dinv[src] * w * dinv[dst]
            return (src, dst, norm)

        def _gcn_conv(x, src, dst, norm, W, b, n_nodes):
            h = x @ W
            msg = h[src] * norm[:, None]
            out = jax.ops.segment_sum(msg, dst, num_segments=n_nodes)
            return out + b
        n = x.shape[0]
        src, dst, norm = _gcn_norm(edge_index, edge_weights, n)
        h = _gcn_conv(x, src, dst, norm, W1, b1, n)
        h = jax.nn.relu(h)
        h = _gcn_conv(h, src, dst, norm, W2, b2, n)
        h = jax.nn.relu(h)
        h = _gcn_conv(h, src, dst, norm, W3, b3, n)
        return h @ Wl + bl

    def _L1_gnn_ref(node_feats, edge_feats, eps, W1, b1, gamma1, beta1, W2, b2, gamma2, beta2, src, dst):
        import jax, jax.numpy as jnp
        import numpy as np
        N_NODES = 10000
        N_EDGES = 10000
        D = 128
        BN_EPS = 1e-05

        def _batchnorm(x, gamma, beta):
            mu = jnp.mean(x, axis=0)
            var = jnp.mean(jnp.square(x - mu), axis=0)
            return (x - mu) * jax.lax.rsqrt(var + BN_EPS) * gamma + beta
        n = node_feats.shape[0]
        m = node_feats[src] + edge_feats
        summed = jax.ops.segment_sum(m, dst, num_segments=n)
        deg = jax.ops.segment_sum(jnp.ones((m.shape[0],), dtype=m.dtype), dst, num_segments=n)
        hv_new = summed / jnp.maximum(deg, 1.0)[:, None]
        h = (1.0 + eps[0]) * node_feats + hv_new
        h = h @ W1 + b1
        h = jax.nn.relu(_batchnorm(h, gamma1, beta1))
        h = h @ W2 + b2
        h = jax.nn.relu(_batchnorm(h, gamma2, beta2))
        return h

    def _L2_gnn_ref(x, edge_index, W_h_weight, W_h_bias):
        import jax, jax.numpy as jnp
        import numpy as np
        N_NODES = 100000
        N_EDGES = 25000
        HIDDEN = 128
        DEPTH = 6
        row, col = (edge_index[0], edge_index[1])
        n = x.shape[0]
        deg = jax.ops.segment_sum(jnp.ones_like(col, dtype=x.dtype), col, num_segments=n)
        deg = jnp.clip(deg, 1.0)[:, None]
        for _ in range(DEPTH):
            agg = jax.ops.segment_sum(x[row], col, num_segments=n)
            message = agg / deg
            message = message @ W_h_weight.T + W_h_bias
            message = jax.nn.relu(message)
            x = x + message
        return x

    def _L3_gnn_ref(x, edge_index, W1, b1, W2, b2):
        import jax, jax.numpy as jnp
        import numpy as np
        N_NODES = 50000
        N_EDGES = 10000
        D_IN = 128
        D_HID = 128
        D_OUT = 128

        def gcn_conv(x, edge_index, W, b, num_nodes):
            loops = jnp.arange(num_nodes, dtype=edge_index.dtype)
            src = jnp.concatenate([edge_index[0], loops])
            dst = jnp.concatenate([edge_index[1], loops])
            deg = jax.ops.segment_sum(jnp.ones_like(dst, dtype=x.dtype), dst, num_segments=num_nodes)
            dinv = jnp.where(deg > 0, jax.lax.rsqrt(deg), 0.0)
            norm = dinv[src] * dinv[dst]
            h = x @ W
            msg = norm[:, None] * h[src]
            out = jax.ops.segment_sum(msg, dst, num_segments=num_nodes)
            return out + b
        h = gcn_conv(x, edge_index, W1, b1, x.shape[0])
        h = jnp.tanh(h)
        return h @ W2 + b2
    edge_index = jnp.stack([src, dst])
    h = jnp.maximum(_layernorm(x, axis=-1), 0.0)
    x = x + _L0_gnn_ref(h, edge_index, edge_weight, L0_gnn_W1, L0_gnn_b1, L0_gnn_W2, L0_gnn_b2, L0_gnn_W3, L0_gnn_b3, L0_gnn_Wl, L0_gnn_bl)
    h = jnp.maximum(_layernorm(x, axis=-1), 0.0)
    x = x + _L1_gnn_ref(h, edge_attr_128, L1_gnn_eps, L1_gnn_W1, L1_gnn_b1, L1_gnn_gamma1, L1_gnn_beta1, L1_gnn_W2, L1_gnn_b2, L1_gnn_gamma2, L1_gnn_beta2, src, dst)
    h = jnp.maximum(_layernorm(x, axis=-1), 0.0)
    x = x + _L2_gnn_ref(h, edge_index, L2_gnn_W_h_weight, L2_gnn_W_h_bias)
    h = jnp.maximum(_layernorm(x, axis=-1), 0.0)
    x = x + _L3_gnn_ref(h, edge_index, L3_gnn_W1, L3_gnn_b1, L3_gnn_W2, L3_gnn_b2)
    return x

_drawn_inputs = setup_inputs


def setup_inputs(seed=0):
    import zlib

    import numpy as np

    out = dict(_drawn_inputs(seed))
    spreads = {'L0_gnn_b1': (0.0, 0.1),
     'L0_gnn_b2': (0.0, 0.1),
     'L0_gnn_b3': (0.0, 0.1),
     'L0_gnn_bl': (0.0, 0.1),
     'L1_gnn_b1': (0.0, 0.8),
     'L1_gnn_gamma1': (1.0, 0.2),
     'L1_gnn_beta1': (0.0, 0.1),
     'L1_gnn_b2': (0.0, 0.8),
     'L1_gnn_gamma2': (1.0, 0.2),
     'L1_gnn_beta2': (0.0, 0.1),
     'L3_gnn_b1': (0.0, 0.308),
     'L3_gnn_b2': (0.0, 0.1)}
    factors = {}
    for name, (base, spread) in spreads.items():
        noise = np.random.default_rng([zlib.crc32(name.encode()), seed]).standard_normal(out[name].shape)
        drawn = base * np.exp(spread * noise) if base else spread * noise
        out[name] = jnp.asarray(drawn.astype(out[name].dtype))
    for name, factor in factors.items():
        out[name] = (out[name] * factor).astype(out[name].dtype)
    return out
```

```python
import concourse.bass as bass
from concourse import mybir
from contextlib import ExitStack
import numpy as np

F32 = mybir.dt.float32
BF16 = mybir.dt.bfloat16
I32 = mybir.dt.int32
ALU = mybir.AluOpType
AF = mybir.ActivationFunctionType

P = 128
D = 128
N = 50000
E = 12500
NT = -(-E // P)
EP = NT * P
SUB = (4, 3)
IT = NT // sum(SUB)
GR = 4 * P
DG = -(-N // GR)
DR = DG * GR
TAILP = (N - (DG - 1) * GR) // 4
RG = -(-EP // GR)
RR = RG * GR
GROUPS = DG + 2 * RG
CONST_ROWS = (DG + RG) * GR - N
LN_EPS = 1e-5
BN_EPS = 1e-5
NO_SLOT = 100000
PAD_NODE = 60000
STEPS = 6
assert NT % sum(SUB) == 0 and DG % 2 == 0 and GROUPS % 2 == 0


def build(nc, x, src, dst, attr, ew, W01, b01, W02, b02, W03, b03, W0l, b0l, eps1, W11, b11, ga1, be1,
          W12, b12, ga2, be2, Wh, bh, W31, b31, W32, b32, out):
    top = ExitStack()

    scopes = [[]]

    def sem(name):
        s = nc.alloc_semaphore(name=name)
        scopes[-1].append(s)
        return s

    def phase():
        scopes.append([])
        return ExitStack()

    def end(ctx):
        ctx.close()
        nc.clear_and_free_semaphores(scopes.pop())
        nc.all_engine_barrier()

    def sems(name, n):
        return [sem(f"{name}{i}") for i in range(n)]

    def after(eng, s, value):
        if not (isinstance(value, int) and value <= 0):
            eng.wait_ge(s, value)

    passed = sem("passed")

    def wait_apart(eng, *waits):
        for s, v in waits:
            after(eng, s, v)
        eng.sem_inc(passed, 1)

    def sb(ctx, name, shape, dt=F32):
        return ctx.enter_context(nc.sbuf_tensor(name, shape, dt))

    def ps(ctx, name):
        return ctx.enter_context(nc.psum_tensor(name, [P, 512], F32))

    def dram(name, shape, dt=F32):
        return nc.dram_tensor(name, shape, dt, kind="Internal").ap()

    def column(v):
        return v.rearrange("(p o) -> p o", o=1)

    def group_rows(table, g):
        return table[bass.ds(g * GR, GR), :].rearrange("(p j) d -> p j d", j=4)

    def edge_rows(table, base, tile, nt):
        return table[bass.ds(tile * P + base, nt * P), :].rearrange("(t p) d -> p t d", p=P)

    def first_tile(i, b):
        return i * sum(SUB) + b * SUB[0]

    node_slot = dram("node_slot", (DR, 1), I32)
    keep_d = dram("keep_d", (1, EP))
    sums_d = dram("sums_d", (2, EP))
    msg_tab = [dram(f"msg_tab{k}", (2 * RR, D)) for k in range(4)]
    step_tab = [dram(f"step_tab{k}", (2 * RR, D)) for k in range(2)]
    last_tab = dram("last_tab", (2 * RR, D))
    x_s = dram("x_s", (EP, D))
    x1_tab = dram("x1_tab", (GROUPS * GR, D))
    x2_tab = dram("x2_tab", (2 * RR, D))
    x3_s = dram("x3_s", (EP, D))
    hin_tab = dram("hin_tab", (GROUPS * GR, D))
    y2_tab = dram("y2_tab", (GROUPS, P, 512))
    E0, S0 = DR, DR + RR

    keep = sb(top, "keep", [P, EP], BF16)
    RS = sb(top, "RS", [P, NT, D])
    RE = sb(top, "RE", [P, NT, D])
    ident = sb(top, "ident", [P, P])
    ones3 = sb(top, "ones3", [3, P], BF16)
    neghalf = sb(top, "neghalf", [P, 2])
    lneps = sb(top, "lneps", [P, 1])
    epsc = sb(top, "epsc", [P, 2])
    w01, w02, w3l, wht, w31, w32 = (sb(top, n, [P, D]) for n in ("w01", "w02", "w3l", "wht", "w31", "w32"))
    w11 = sb(top, "w11", [P, 2 * D])
    w12 = sb(top, "w12", [P, 2, D])
    col = sb(top, "col", [P, 12])
    C_B01, C_B02, C_B31, C_B12, C_GA2, C_BE2, C_B11, C_GA1, C_BE1 = 0, 1, 2, 3, 4, 5, 6, 8, 10
    rb01, rb02, rb3l, rbh, rb31, rb32, r6 = (sb(top, n, [P, D]) for n in
                                             ("rb01", "rb02", "rb3l", "rbh", "rb31", "rb32", "r6"))
    rmsg = sb(top, "rmsg", [P, D])
    split_x1 = sb(top, "split_x1", [3, 512], BF16)
    split_out = sb(top, "split_out", [3, 512], BF16)
    wE = sb(top, "wE", [P, NT])
    isend = sb(top, "isend", [P, NT])
    dinvw = sb(top, "dinvw", [P, NT])
    uw = sb(top, "uw", [P, NT])
    cnt = sb(top, "cnt", [P, NT])
    inv_cnt = sb(top, "inv_cnt", [P, NT])
    inv_end = sb(top, "inv_end", [P, NT])
    vscale = sb(top, "vscale", [P, NT])
    dinvu = sb(top, "dinvu", [P, NT])
    uu = sb(top, "uu", [P, NT])
    src_i = sb(top, "src_i", [P, NT], I32)
    dst_i = sb(top, "dst_i", [P, NT], I32)
    end_i = sb(top, "end_i", [P, NT], I32)
    row_i = sb(top, "row_i", [P, NT], I32)
    maskd = sb(top, "maskd", [P, DG, 4])
    gram = sb(top, "gram", [P, 130])
    bn1 = sb(top, "bn1", [P, 4])
    bn2 = sb(top, "bn2", [P, 2])

    ctx = phase()
    ed = {n: sb(ctx, n, [NT, P], I32) for n in ("ed_a", "ed_n", "ed_p", "ed_s")}
    ef = {n: sb(ctx, n, [NT, P]) for n in ("ef_a", "ef_n", "ef_p", "ef_s", "ef_w", "ef_end", "ef_keep",
                                           "ef_sw", "ef_cn")}
    fill = sb(ctx, "fill", [DG, 508], I32)
    zero_i = sb(ctx, "zero_i", [1, 512], I32)
    keepf = sb(ctx, "keepf", [2, EP // 8])
    e_io = sb(ctx, "e_io", [P, NT], I32)
    ef32 = sb(ctx, "ef32", [P, NT])
    slot = sb(ctx, "slot", [P, NT], I32)
    t1, t2, t3 = (sb(ctx, n, [P, NT]) for n in ("t1", "t2", "t3"))
    w3t, w3, wl, whs = (sb(ctx, n, [P, D]) for n in ("w3t", "w3", "wl", "whs"))
    b3col = sb(ctx, "b3col", [P, 1])
    b3bc = sb(ctx, "b3bc", [P, P])
    rbl = sb(ctx, "rbl", [P, D])
    zrow = sb(ctx, "zrow", [P, 2, D])
    node_p = sb(ctx, "node_p", [DG, 512], I32)
    node_f = sb(ctx, "node_f", [DG, 512])
    sp_h, sp_m, sp_l = (sb(ctx, n, [1, 2, D], BF16) for n in ("sp_h", "sp_m", "sp_l"))
    sp_f, sp_r = (sb(ctx, n, [1, 2, D]) for n in ("sp_f", "sp_r"))
    runs2 = RS[0:2, :, :].rearrange("p t d -> p (t d)")
    vals2 = RE[0:2, :, :].rearrange("p t d -> p (t d)")
    keep2 = keep[0:2, :]
    pA, pB, pC = ps(ctx, "s_pA"), ps(ctx, "s_pB"), ps(ctx, "s_pC")
    pD = ps(ctx, "s_pD")
    filled, edges_in, weights_in, zeroed = sem("filled"), sem("edges_in"), sem("weights_in"), sem("zeroed")
    pool_s, dve_s, pe_s, act_s = sem("pool_s"), sem("dve_s"), sem("pe_s"), sem("act_s")
    keep_st, keep_ld, sums_st, sums_ld = sem("keep_st"), sem("keep_ld"), sem("sums_st"), sem("sums_ld")
    dve_own = sem("dve_own")
    tab_init, slots_set, slot_got, node_in, split_in = (sem("tab_init"), sem("slots_set"), sem("slot_got"),
                                                        sem("node_in"), sem("split_in"))
    N_LOADS = 30
    FULL = NT - 1
    REST = E - FULL * P

    with nc.Block() as block:
        @block.sync
        def _(sp):
            loads = [(w01[:, :], W01[:, :]), (w02[:, :], W02[:, :]), (w3[:, :], W03[:, :]), (wl[:, :], W0l[:, :]),
                     (whs[:, :], Wh[:, :]), (w31[:, :], W31[:, :]), (w32[:, :], W32[:, :]), (w11[:, :], W11[:, :]),
                     (w12[:, :, :], W12.rearrange("(c p) n -> p c n", p=P)), (b3col[:, :], column(b03)),
                     (rb01[:, :], b01.partition_broadcast(P)), (rb02[:, :], b02.partition_broadcast(P)),
                     (rbl[:, :], b0l.partition_broadcast(P)), (rbh[:, :], bh.partition_broadcast(P)),
                     (rb31[:, :], b31.partition_broadcast(P)), (rb32[:, :], b32.partition_broadcast(P)),
                     (epsc[:, 0:1], eps1.partition_broadcast(P)),
                     (sp_f[0:1, 1, :], b32.rearrange("(o n) -> o n", o=1))]
            for c, v in ((C_B01, b01), (C_B02, b02), (C_B31, b31), (C_B12, b12), (C_GA2, ga2), (C_BE2, be2)):
                loads.append((col[:, c:c + 1], column(v)))
            for c, v in ((C_B11, b11), (C_GA1, ga1), (C_BE1, be1)):
                for half in range(2):
                    loads.append((col[:, c + half:c + half + 1], column(v[half * P:(half + 1) * P])))
            sp.wait_ge(filled, 1)
            for name, lo in (("ed_a", 0), ("ed_n", 1)):
                sp.dma_start(ed[name][0:FULL, :], dst[lo:lo + FULL * P].rearrange("(t p) -> t p", p=P)).then_inc(edges_in, 16)
                sp.dma_start(ed[name][FULL:NT, 0:REST - lo], dst[FULL * P + lo:E].rearrange("(o p) -> o p", o=1)).then_inc(edges_in, 16)
            sp.dma_start(ed["ed_p"][0:1, 1:P], dst[0:P - 1].rearrange("(o p) -> o p", o=1)).then_inc(edges_in, 16)
            sp.dma_start(ed["ed_p"][1:FULL, :], dst[P - 1:P - 1 + (FULL - 1) * P].rearrange("(t p) -> t p", p=P)).then_inc(edges_in, 16)
            sp.dma_start(ed["ed_p"][FULL:NT, 0:REST], dst[FULL * P - 1:E - 1].rearrange("(o p) -> o p", o=1)).then_inc(edges_in, 16)
            sp.dma_start(ed["ed_s"][0:FULL, :], src[0:FULL * P].rearrange("(t p) -> t p", p=P)).then_inc(edges_in, 16)
            sp.dma_start(ed["ed_s"][FULL:NT, 0:REST], src[FULL * P:E].rearrange("(o p) -> o p", o=1)).then_inc(edges_in, 16)
            sp.dma_start(ef["ef_w"][0:FULL, :], ew[0:FULL * P].rearrange("(t p) -> t p", p=P)).then_inc(edges_in, 16)
            sp.dma_start(ef["ef_w"][FULL:NT, 0:REST], ew[FULL * P:E].rearrange("(o p) -> o p", o=1)).then_inc(edges_in, 16)
            sp.dma_start(vals2[0:1, 0:E], ew.rearrange("(o p) -> o p", o=1)).then_inc(edges_in, 16)
            sp.dma_start(node_slot[0:DG * 508, :].rearrange("(p c) o -> p (c o)", p=DG), fill[:, :]).then_inc(tab_init, 16)
            sp.dma_start(node_slot[DG * 508:N, :].rearrange("(p c) o -> p (c o)", p=1), fill[0:1, 0:N - DG * 508]).then_inc(tab_init, 16)
            sp.dma_start(node_slot[N:DR, :].rearrange("(p c) o -> p (c o)", p=1), zero_i[0:1, 0:DR - N]).then_inc(tab_init, 16)
            assert len(loads) == N_LOADS
            for o, i in loads:
                sp.dma_start(o, i).then_inc(weights_in, 16)
            padded = [(hin_tab, E0), (hin_tab, S0), (x1_tab, E0), (x1_tab, S0)]
            padded += [(t, base) for t in msg_tab + step_tab + [last_tab] for base in (0, RR)]
            for t, base in padded:
                sp.dma_start(t[base + EP:base + RR, :].rearrange("(p j) d -> p j d", p=P), zrow[:, :, :]).then_inc(zeroed, 16)
            sp.wait_ge(dve_s, 2)
            sp.dma_start(keep_d.rearrange("o (t p) -> (o t) p", p=P), ef["ef_keep"][:, :]).then_inc(keep_st, 16)
            sp.wait_ge(dve_s, 3)
            sp.dma_start(sums_d[:, :], runs2).then_inc(sums_st, 16)
            sp.wait_ge(sums_st, 16)
            sp.dma_start(ef["ef_sw"][:, :], sums_d[0:1, :].rearrange("o (t p) -> (o t) p", p=P)).then_inc(sums_ld, 16)
            sp.dma_start(ef["ef_cn"][:, :], sums_d[1:2, :].rearrange("o (t p) -> (o t) p", p=P)).then_inc(sums_ld, 16)
            sp.wait_ge(dve_s, 9)
            for k, part in enumerate((sp_h, sp_m, sp_l)):
                for which, split in enumerate((split_x1, split_out)):
                    for r in range(4):
                        sp.dma_start(split[k:k + 1, r * D:(r + 1) * D], part[0:1, which, :]).then_inc(split_in, 16)
            sp.wait_ge(slots_set, 16 * NT)
            sp.dma_start(node_p[:, :], node_slot.rearrange("(g c) o -> g (c o)", g=DG)).then_inc(node_in, 16)
            sp.wait_ge(zeroed, 16 * len(padded))
            sp.wait_ge(split_in, 16 * 24)

        @block.gpsimd
        def _(pool):
            nc.gpsimd.memset(ed["ed_a"][:, :], PAD_NODE)
            nc.gpsimd.memset(ed["ed_n"][:, :], PAD_NODE)
            nc.gpsimd.memset(ed["ed_p"][:, :], -1)
            nc.gpsimd.memset(ed["ed_s"][:, :], 0)
            nc.gpsimd.memset(ef["ef_w"][:, :], 0.0)
            nc.gpsimd.memset(vals2, 1.0)
            nc.gpsimd.memset(zrow[:, :, :], 0.0)
            nc.gpsimd.memset(zero_i[:, :], 0)
            nc.gpsimd.memset(fill[:, :], NO_SLOT).then_inc(filled, 1)
            nc.gpsimd.memset(ones3[:, :], 1.0)
            nc.gpsimd.memset(neghalf[:, :], -0.5)
            nc.gpsimd.memset(lneps[:, :], LN_EPS)
            nc.gpsimd.iota(e_io[:, :], pattern=[[P, NT]], base=0, channel_multiplier=1)
            nc.gpsimd.memset(ident[:, :], 0.0).then_inc(pool_s, 1)
            pool.wait_ge(pool_s, 1)
            nc.gpsimd.affine_select(out=ident[:, :], in_=ident[:, :], compare_op=ALU.not_equal, fill=1.0,
                                    base=0, pattern=[[-1, P]], channel_multiplier=1).then_inc(pool_s, 1)
            pool.wait_ge(keep_st, 16)
            pool.dma_start(keep[:, :], keep_d[0, :].partition_broadcast(P)).then_inc(keep_ld, 16)
            pool.wait_ge(tab_init, 48)
            pool.wait_ge(dve_s, 5)
            for t in range(NT):
                pool.indirect_dma_start(out=node_slot[:, :], out_offset=bass.IndirectOffsetOnAxis(ap=end_i[:, t:t + 1], axis=0),
                                        in_=e_io[:, t:t + 1], in_offset=None, bounds_check=N - 1,
                                        oob_is_err=False).then_inc(slots_set, 16)
            pool.wait_ge(slots_set, 16 * NT)
            for t in range(NT):
                pool.indirect_dma_start(out=slot[:, t:t + 1], out_offset=None, in_=node_slot[:, :],
                                        in_offset=bass.IndirectOffsetOnAxis(ap=src_i[:, t:t + 1], axis=0)).then_inc(slot_got, 16)
            pool.wait_ge(slot_got, 16 * NT)

        @block.tensor
        def _(pe):
            pe.wait_ge(pool_s, 2)
            pe.wait_ge(dve_s, 2)
            for k, name in enumerate(("ef_a", "ef_end", "ef_s", "ef_w")):
                last = nc.tensor.transpose(pA[:, k * P:k * P + NT], ef[name][:, :], ident[0:NT, 0:NT])
            last.then_inc(pe_s, 1)
            pe.wait_ge(sums_ld, 32)
            nc.tensor.transpose(pB[:, 0:NT], ef["ef_sw"][:, :], ident[0:NT, 0:NT])
            nc.tensor.transpose(pB[:, P:P + NT], ef["ef_cn"][:, :], ident[0:NT, 0:NT]).then_inc(pe_s, 1)
            pe.wait_ge(weights_in, 16 * N_LOADS)
            nc.tensor.transpose(pC[:, 0:P], w3[:, :], ident[:, :])
            nc.tensor.transpose(pC[:, P:2 * P], whs[:, :], ident[:, :]).then_inc(pe_s, 1)
            pe.wait_ge(act_s, 2)
            nc.tensor.matmul(pC[:, 2 * P:3 * P], w3t[:, :], wl[:, :], start=True, stop=True)
            nc.tensor.matmul(pC[:, 3 * P:4 * P], b3bc[:, :], wl[:, :], start=True, stop=True).then_inc(pe_s, 1)
            pe.wait_ge(dve_s, 11)
            for j in range(4):
                last = nc.tensor.transpose(pD[:, j * P:j * P + DG], node_f[:, :].rearrange("g (p j) -> g j p", j=4)[:, j, :],
                                           ident[0:DG, 0:DG])
            last.then_inc(pe_s, 1)

        @block.scalar
        def _(act):
            act.wait_ge(pe_s, 3)
            nc.scalar.activation(w3t[:, :], pC[:, 0:P], AF.Copy)
            nc.scalar.activation(wht[:, :], pC[:, P:2 * P], AF.Copy).then_inc(act_s, 1)
            act.wait_ge(act_s, 1)
            act.wait_ge(weights_in, 16 * N_LOADS)
            nc.scalar.activation(b3bc[:, :], ident[:, :], AF.Identity, bias=b3col[:, :], scale=0.0).then_inc(act_s, 1)
            act.wait_ge(pe_s, 4)
            nc.scalar.activation(w3l[:, :], pC[:, 2 * P:3 * P], AF.Copy).then_inc(act_s, 1)
            act.wait_ge(dve_s, 6)
            nc.scalar.activation(t3[:, :], t1[:, :], AF.Sqrt)
            nc.scalar.activation(ef32[:, :], t2[:, :], AF.Sqrt).then_inc(act_s, 1)

        @block.vector
        def _(dve):
            own = [0]

            def step(ins):
                own[0] += 1
                ins.then_inc(dve_own, 1)
                dve.wait_ge(dve_own, own[0])

            dve.wait_ge(edges_in, 16 * 12)
            nc.vector.tensor_copy(ef["ef_a"][:, :], ed["ed_a"][:, :])
            nc.vector.tensor_copy(ef["ef_n"][:, :], ed["ed_n"][:, :])
            nc.vector.tensor_copy(ef["ef_s"][:, :], ed["ed_s"][:, :])
            nc.vector.tensor_copy(ef["ef_p"][:, :], ed["ed_p"][:, :]).then_inc(dve_s, 1)
            dve.wait_ge(dve_s, 1)
            nc.vector.tensor_tensor(ef["ef_end"][:, :], ef["ef_n"][:, :], ef["ef_a"][:, :], ALU.not_equal)
            nc.vector.tensor_tensor(ef["ef_keep"][:, :], ef["ef_p"][:, :], ef["ef_a"][:, :], ALU.is_equal).then_inc(dve_s, 1)
            dve.wait_ge(keep_ld, 16)
            nc.vector.tensor_tensor_scan(runs2, keep2, vals2, 0.0, ALU.mult, ALU.add).then_inc(dve_s, 1)
            dve.wait_ge(pe_s, 1)
            nc.vector.tensor_copy(isend[:, :], pA[:, P:P + NT])
            nc.vector.tensor_copy(src_i[:, :], pA[:, 2 * P:2 * P + NT])
            nc.vector.tensor_scalar(dst_i[:, :], pA[:, 0:NT], float(N - 1), None, ALU.min)
            step(nc.vector.tensor_copy(wE[:, :], pA[:, 3 * P:3 * P + NT]))
            nc.vector.tensor_scalar(t1[:, :], pA[:, 0:NT], -float(NO_SLOT), None, ALU.add).then_inc(dve_s, 1)
            dve.wait_ge(dve_s, 4)
            step(nc.vector.tensor_tensor(t2[:, :], t1[:, :], isend[:, :], ALU.mult))
            nc.vector.tensor_scalar(end_i[:, :], t2[:, :], float(NO_SLOT), None, ALU.add).then_inc(dve_s, 1)
            dve.wait_ge(pe_s, 2)
            dve.wait_ge(dve_s, 5)
            nc.vector.tensor_copy(cnt[:, :], pB[:, P:P + NT])
            step(nc.vector.tensor_scalar(inv_end[:, :], pB[:, 0:NT], 1.0, None, ALU.add))
            step(nc.vector.tensor_scalar(uw[:, :], inv_end[:, :], 0.0, None, ALU.is_gt))
            nc.vector.tensor_scalar(t1[:, :], inv_end[:, :], 1e-30, None, ALU.max)
            nc.vector.tensor_scalar(t2[:, :], cnt[:, :], 1.0, None, ALU.add).then_inc(dve_s, 1)
            dve.wait_ge(dve_s, 6)
            step(nc.vector.reciprocal(inv_cnt[:, :], cnt[:, :]))
            step(nc.vector.tensor_tensor(inv_end[:, :], inv_cnt[:, :], isend[:, :], ALU.mult))
            dve.wait_ge(weights_in, 16 * N_LOADS)
            step(nc.vector.tensor_scalar(epsc[:, 1:2], epsc[:, 0:1], 1.0, None, ALU.add))
            step(nc.vector.tensor_tensor(vscale[:, :], cnt[:, :], isend[:, :], ALU.mult))
            nc.vector.tensor_scalar(vscale[:, :], vscale[:, :], epsc[:, 1:2], None, ALU.mult)
            dve.wait_ge(act_s, 4)
            nc.vector.reciprocal(dinvu[:, :], ef32[:, :])
            step(nc.vector.reciprocal(t2[:, :], t3[:, :]))
            step(nc.vector.tensor_tensor(dinvw[:, :], t2[:, :], uw[:, :], ALU.mult))
            nc.vector.tensor_tensor(uw[:, :], dinvw[:, :], isend[:, :], ALU.mult)
            nc.vector.tensor_tensor(uu[:, :], dinvu[:, :], isend[:, :], ALU.mult).then_inc(dve_s, 1)
            dve.wait_ge(pe_s, 4)
            dve.wait_ge(act_s, 3)
            nc.vector.tensor_tensor(rb3l[:, :], pC[:, 3 * P:4 * P], rbl[:, :], ALU.add)
            step(nc.vector.tensor_scalar(rmsg[:, :], rbh[:, :], 0.0, None, ALU.max))
            step(nc.vector.tensor_scalar(r6[:, :], rmsg[:, :], float(STEPS), None, ALU.mult))
            nc.vector.tensor_copy(sp_f[0:1, 0, :], rb3l[0:1, :]).then_inc(dve_s, 1)
            dve.wait_ge(dve_s, 8)
            step(nc.vector.tensor_copy(sp_h[:, :, :], sp_f[:, :, :]))
            step(nc.vector.tensor_tensor(sp_r[:, :, :], sp_f[:, :, :], sp_h[:, :, :], ALU.subtract))
            step(nc.vector.tensor_copy(sp_m[:, :, :], sp_r[:, :, :]))
            step(nc.vector.tensor_tensor(sp_r[:, :, :], sp_r[:, :, :], sp_m[:, :, :], ALU.subtract))
            nc.vector.tensor_copy(sp_l[:, :, :], sp_r[:, :, :]).then_inc(dve_s, 1)
            dve.wait_ge(slot_got, 16 * NT)
            nc.vector.tensor_copy(ef32[:, :], e_io[:, :])
            step(nc.vector.tensor_copy(t1[:, :], slot[:, :]))
            nc.vector.tensor_scalar(t2[:, :], t1[:, :], float(EP), None, ALU.is_lt)
            step(nc.vector.tensor_scalar(t3[:, :], t1[:, :], float(RR), None, ALU.add))
            step(nc.vector.tensor_tensor(t3[:, :], t3[:, :], ef32[:, :], ALU.subtract))
            step(nc.vector.tensor_tensor(t3[:, :], t3[:, :], t2[:, :], ALU.mult))
            nc.vector.tensor_tensor(row_i[:, :], t3[:, :], ef32[:, :], ALU.add).then_inc(dve_s, 1)
            dve.wait_ge(node_in, 16)
            nc.vector.tensor_scalar(node_f[:, :], node_p[:, :], float(EP), None, ALU.is_gt).then_inc(dve_s, 1)
            dve.wait_ge(pe_s, 5)
            for j in range(4):
                nc.vector.tensor_copy(maskd[:, :, j], pD[:, j * P:j * P + DG])
            dve.drain()
    end(ctx)

    class Norm:

        def __init__(self, ctx, tag, on_act=False):
            self.on_act = on_act
            self.st = [sb(ctx, f"{tag}_st{b}", [P, 4, 6]) for b in range(2)]
            self.mv = [sb(ctx, f"{tag}_mv{b}", [P, 4, 2]) for b in range(2)]
            self.sd = [sb(ctx, f"{tag}_sd{b}", [P, 4]) for b in range(2)]
            self.r0 = [sb(ctx, f"{tag}_r0{b}", [P, 4]) for b in range(2)]
            self.rs = [sb(ctx, f"{tag}_rs{b}", [P, 4]) for b in range(2)]
            self.nm = [sb(ctx, f"{tag}_nm{b}", [P, 4]) for b in range(2)]
            self.stats, self.moments, self.std = sem(f"{tag}_stats"), sem(f"{tag}_moments"), sem(f"{tag}_std")
            self.rstd0, self.rstd, self.normed = sem(f"{tag}_rstd0"), sem(f"{tag}_rstd"), sem(f"{tag}_normed")
            self.shifted = sem(f"{tag}_shifted") if on_act else self.normed

        def dve_moments(self, dve, q, b, nt, rows):
            after(dve, self.moments, q - 1)
            for j in range(nt):
                last = nc.vector.bn_stats(self.st[b][:, j, :], rows[:, j, :])
            last.then_inc(self.stats, 1)
            wait_apart(dve, (self.stats, q + 1),
                       (self.shifted, q - 1))
            for j in range(nt):
                last = nc.vector.bn_aggr(self.mv[b][:, j, :], self.st[b][:, j, :])
            last.then_inc(self.moments, 1)

        def act_std(self, act, q, b, nt):
            act.wait_ge(self.moments, q + 1)
            after(act, self.rstd, q - 1)
            nc.scalar.activation(self.sd[b][:, 0:nt], self.mv[b][:, 0:nt, 1], AF.Sqrt, bias=lneps[:, 0:1]).then_inc(self.std, 1)

        def dve_rstd(self, dve, q, b, nt, mask=None):
            dve.wait_ge(self.std, q + 1)
            after(dve, self.normed, q - 1)
            if mask is not None:
                nc.vector.reciprocal(self.r0[b][:, 0:nt], self.sd[b][:, 0:nt]).then_inc(self.rstd0, 1)
                dve.wait_ge(self.rstd0, q + 1)
                nc.vector.tensor_tensor(self.rs[b][:, 0:nt], self.r0[b][:, 0:nt], mask, ALU.mult).then_inc(self.rstd, 1)
            else:
                nc.vector.reciprocal(self.rs[b][:, 0:nt], self.sd[b][:, 0:nt]).then_inc(self.rstd, 1)
            if self.on_act:
                dve.wait_ge(self.rstd, q + 1)
                nc.vector.scalar_tensor_tensor(self.nm[b][:, 0:nt], self.mv[b][:, 0:nt, 0], -1.0, self.rs[b][:, 0:nt],
                                               ALU.mult, ALU.mult).then_inc(self.shifted, 1)

        def dve_apply(self, dve, q, b, nt, rows, normed):
            dve.wait_ge(self.rstd, q + 1)
            for j in range(nt):
                last = nc.vector.tensor_scalar(normed[:, j, :], rows[:, j, :], self.mv[b][:, j, 0:1], self.rs[b][:, j:j + 1],
                                               ALU.subtract, ALU.mult)
            last.then_inc(self.normed, 1)

        def act_apply(self, act, q, b, nt, rows, normed):
            act.wait_ge(self.shifted, q + 1)
            for j in range(nt):
                last = nc.scalar.activation(normed[:, j, :], rows[:, j, :], AF.Relu, scale=self.rs[b][:, j:j + 1],
                                            bias=self.nm[b][:, j:j + 1])
            last.then_inc(self.normed, 1)

    ctx = phase()
    X = [sb(ctx, f"s_x{k}", [P, 4, D]) for k in range(4)]
    ix = [sb(ctx, f"s_ix{b}", [P, 4], I32) for b in range(2)]
    ln = Norm(ctx, "s_ln", on_act=True)
    s_ix, s_got, s_xst, s_ust = sem("s_ix"), sems("s_got", 4), sems("s_xst", 4), sems("s_ust", 2)

    def peeled(eng, n, body):
        body(0)
        with eng.Fori(1, n) as i:
            body(i)

    def peeled2(eng, n, body):
        body(0, 0, 0)
        body(1, 0, 1)
        with eng.Fori(1, n // 2) as k:
            for u in range(2):
                body(2 * k + u, k, u)

    with nc.Block() as block:
        @block.gpsimd
        def _(pool):
            def it(i, k, u):
                for b, nt in enumerate(SUB):
                    q, t, r = 2 * i + b, first_tile(i, b), 2 * u + b
                    after(pool, ln.normed, q - 3)
                    after(pool, s_xst[r], 16 * k)
                    after(pool, s_got[2 * (1 - u) + b], 16 * nt * (k + u))
                    nc.gpsimd.tensor_copy(ix[b][:, 0:nt], dst_i[:, bass.ds(t, nt)]).then_inc(s_ix, 1)
                    wait_apart(pool, (s_ix, q + 1))
                    for j in range(nt):
                        pool.indirect_dma_start(out=X[r][:, j, :], out_offset=None, in_=x[:, :],
                                                in_offset=bass.IndirectOffsetOnAxis(ap=ix[b][:, j:j + 1], axis=0)).then_inc(s_got[r], 16)
            peeled2(pool, IT, it)

        @block.vector
        def _(dve):
            def it(i, k, u):
                for b, nt in enumerate(SUB):
                    dve.wait_ge(s_got[2 * u + b], 16 * nt * (k + 1))
                    ln.dve_moments(dve, 2 * i + b, b, nt, X[2 * u + b])
                for b, nt in enumerate(SUB):
                    ln.dve_rstd(dve, 2 * i + b, b, nt, mask=uw[:, bass.ds(first_tile(i, b), nt)])
            peeled2(dve, IT, it)

        @block.scalar
        def _(act):
            def it(i, k, u):
                for b, nt in enumerate(SUB):
                    ln.act_std(act, 2 * i + b, b, nt)
                for b, nt in enumerate(SUB):
                    ln.act_apply(act, 2 * i + b, b, nt, X[2 * u + b], _Rows(RS, first_tile(i, b)))
            peeled2(act, IT, it)

        @block.sync
        def _(sp):
            def it(i, k, u):
                for b, nt in enumerate(SUB):
                    r = 2 * u + b
                    sp.wait_ge(s_got[r], 16 * nt * (k + 1))
                    sp.dma_start(edge_rows(x_s, 0, first_tile(i, b), nt), X[r][:, 0:nt, :]).then_inc(s_xst[r], 16)
                for b, nt in enumerate(SUB):
                    t = first_tile(i, b)
                    sp.wait_ge(ln.normed, 2 * i + b + 1)
                    sp.dma_start(edge_rows(msg_tab[0], RR, t, nt), RS[:, bass.ds(t, nt), :]).then_inc(s_ust[b], 16)
            peeled2(sp, IT, it)
            for b in range(2):
                sp.wait_ge(s_ust[b], 16 * IT)
            for r in range(4):
                sp.wait_ge(s_xst[r], 16 * IT // 2)
    end(ctx)

    class Chain:

        def __init__(self, ctx, tag, ring, widths, gram):
            self.widths, self.gram = widths, gram
            self.stores = 16 if gram else 32
            two = lambda n, shape: [sb(ctx, f"{tag}_{n}{b}", shape) for b in range(2)]
            self.X = [sb(ctx, f"{tag}_X{k}", [P, 4, D]) for k in range(ring)]
            self.NR, self.H0, self.H1, self.H2 = (two(n, [P, 4, D]) for n in ("NR", "H0", "H1", "H2"))
            self.X1 = two("X1", [P, 4, D])
            self.HI = two("HI", [P, 4, 130])
            self.PA = [ps(ctx, f"{tag}_PA{b}") for b in range(2)]
            self.P3 = [ps(ctx, f"{tag}_P3{b}") for b in range(2)]
            self.ln1, self.ln2 = Norm(ctx, f"{tag}_ln1"), Norm(ctx, f"{tag}_ln2", on_act=True)
            self.hin = self.ln2.normed
            self.x_in = sems(f"{tag}_x_in", ring)
            self.t0, self.e0, self.m1, self.e1, self.m2, self.e2, self.m3 = (
                sem(f"{tag}_{n}") for n in ("rows_turned", "h0_set", "prod1", "h1_set", "prod2", "h2_set", "prod3"))
            self.x1, self.gr = sem(f"{tag}_x1_set"), sem(f"{tag}_gram_added")
            self.x1_st, self.hin_st = sems(f"{tag}_x1_st", 2), sems(f"{tag}_hin_st", 2)

        def pe_turn(self, pe, j, b):
            q, nt = 2 * j + b, self.widths[b]
            pe.wait_ge(self.ln1.normed, q + 1)
            after(pe, self.e2, q - 1)
            for k in range(nt):
                last = nc.tensor.transpose(self.PA[b][:, k * P:(k + 1) * P], self.NR[b][:, k, :], ident[:, :])
            last.then_inc(self.t0, 1)

        def act_h0(self, act, j, b):
            q, w = 2 * j + b, self.widths[b]
            act.wait_ge(self.t0, q + 1)
            after(act, self.m1, q - 1)
            nc.scalar.activation(self.H0[b][:, 0:w, :], self.PA[b][:, 0:w * P], AF.Relu).then_inc(self.e0, 1)

        def pe_prod(self, pe, j, b, which):
            w, h, ready, done = ((w01, self.H0, self.e0, self.m1), (w02, self.H1, self.e1, self.m2))[which]
            q = 2 * j + b
            pe.wait_ge(ready, q + 1)
            nc.tensor.matmul(self.PA[b][:, 0:self.widths[b] * P], w[:, :],
                             h[b][:, 0:self.widths[b], :].rearrange("p t d -> p (t d)"), start=True, stop=True).then_inc(done, 1)

        def act_h(self, act, j, b, which, read=None):
            h, c, ready, done, used = ((self.H1, C_B01, self.m1, self.e1, self.m2),
                                       (self.H2, C_B02, self.m2, self.e2, self.m3))[which]
            q, w = 2 * j + b, self.widths[b]
            act.wait_ge(ready, q + 1)
            after(act, used, q - 1)
            if read is not None:
                after(act, read, q - 1)
            nc.scalar.activation(h[b][:, 0:w, :], self.PA[b][:, 0:w * P], AF.Relu, bias=col[:, c:c + 1]).then_inc(done, 1)

        def pe_rows(self, pe, j, b):
            q, nt = 2 * j + b, self.widths[b]
            pe.wait_ge(self.e2, q + 1)
            after(pe, self.x1, q - 1)
            nc.tensor.matmul(self.P3[b][:, 0:nt * P], ones3[:, :], split_x1[:, 0:nt * P], start=True, stop=False)
            for k in range(nt):
                last = nc.tensor.matmul(self.P3[b][:, k * P:(k + 1) * P], self.H2[b][:, k, :], w3l[:, :],
                                        start=False, stop=(k == nt - 1))
            last.then_inc(self.m3, 1)

        def dve_x1(self, dve, j, b, s):
            q, nt = 2 * j + b, self.widths[b]
            dve.wait_ge(self.m3, q + 1)
            after(dve, self.x1_st[b], 16 * j)
            after(dve, self.hin, q - 1)
            nc.vector.tensor_tensor(self.X1[b][:, 0:nt, :], self.X[2 * s + b][:, 0:nt, :],
                                    self.P3[b][:, 0:nt * P].rearrange("p (t d) -> p t d", d=D), ALU.add).then_inc(self.x1, 1)
            dve.wait_ge(self.x1, q + 1)
            self.ln2.dve_moments(dve, q, b, nt, self.X1[b])

        def act_hin(self, act, j, b):
            q, nt = 2 * j + b, self.widths[b]
            after(act, self.hin_st[b], self.stores * j)
            if self.gram:
                after(act, self.gr, q - 1)
            self.ln2.act_apply(act, q, b, nt, self.X1[b], self.HI[b][:, :, 0:D])

    ctx = phase()
    ch = Chain(ctx, "e", 4, SUB, gram=False)
    ix = [sb(ctx, f"e_ix{b}", [P, 4], I32) for b in range(2)]
    R = [[sb(ctx, f"e_R{k}{b}", [P, 4, D]) for b in range(2)] for k in range(3)]
    PR = [ps(ctx, f"e_PR{b}") for b in range(2)]
    e_ix, r_set = sem("e_ix"), sems("e_r_set", 3)
    r_st = [sems(f"e_r{k}_st", 2) for k in range(3)]
    turned = sems("e_h_turned", 2)

    def peeled2x(eng, n, body):
        body(0, 0, 0)
        body(1, 0, 1)
        with eng.Fori(1, n // 2 - 1) as k:
            for u in range(2):
                body(2 * k + u, k, u)
        body(n - 2, n // 2 - 1, 0)
        body(n - 1, n // 2 - 1, 1)

    with nc.Block() as block:
        @block.gpsimd
        def _(pool):
            def it(i, k, u):
                for b, nt in enumerate(SUB):
                    q, t, r = 2 * i + b, first_tile(i, b), 2 * u + b
                    after(pool, ch.x1, q - 3)
                    after(pool, ch.x_in[2 * (1 - u) + b], 16 * nt * (k + u))
                    nc.gpsimd.tensor_copy(ix[b][:, 0:nt], src_i[:, bass.ds(t, nt)]).then_inc(e_ix, 1)
                    wait_apart(pool, (e_ix, q + 1))
                    for j in range(nt):
                        pool.indirect_dma_start(out=ch.X[r][:, j, :], out_offset=None, in_=x[:, :],
                                                in_offset=bass.IndirectOffsetOnAxis(ap=ix[b][:, j:j + 1], axis=0)).then_inc(ch.x_in[r], 16)
            peeled2(pool, IT, it)

        @block.vector
        def _(dve):
            def moments(i, k, u):
                for b, nt in enumerate(SUB):
                    dve.wait_ge(ch.x_in[2 * u + b], 16 * nt * (k + 1))
                    ch.ln1.dve_moments(dve, 2 * i + b, b, nt, ch.X[2 * u + b])

            def apply(i, u):
                for b, nt in enumerate(SUB):
                    q = 2 * i + b
                    ch.ln1.dve_rstd(dve, q, b, nt)
                    after(dve, ch.t0, q - 1)
                    after(dve, r_set[0], q - 1)
                    ch.ln1.dve_apply(dve, q, b, nt, ch.X[2 * u + b], ch.NR[b])

            def it(i, k, u):
                last = isinstance(i, int) and i == IT - 1
                if not last:
                    moments(i + 1, k + u, 1 - u)
                    apply(i + 1, 1 - u)
                for b in range(2):
                    ch.dve_x1(dve, i, b, u)
                for b, nt in enumerate(SUB):
                    ch.ln2.dve_rstd(dve, 2 * i + b, b, nt)
                for b, nt in enumerate(SUB):
                    q = 2 * i + b
                    dve.wait_ge(turned[1], q + 1)
                    after(dve, r_st[2][b], 16 * i)
                    nc.vector.tensor_copy(R[2][b][:, 0:nt, :], PR[b][:, 0:nt * P].rearrange("p (t d) -> p t d", d=D)).then_inc(r_set[2], 1)
            moments(0, 0, 0)
            apply(0, 0)
            peeled2x(dve, IT, it)

        @block.tensor
        def _(pe):
            def back(i, b, which):
                q, nt = 2 * i + b, SUB[b]
                h, ready = ((ch.H1, ch.e1), (ch.H2, ch.e2))[which]
                pe.wait_ge(ready, q + 1)
                if which:
                    pe.wait_ge(r_set[1], q + 1)
                else:
                    after(pe, r_set[2], q - 1)
                for k in range(nt):
                    last = nc.tensor.transpose(PR[b][:, k * P:(k + 1) * P], h[b][:, k, :], ident[:, :])
                last.then_inc(turned[which], 1)

            def it(i):
                for b in range(2):
                    ch.pe_turn(pe, i, b)
                for b in range(2):
                    ch.pe_prod(pe, i, b, 0)
                for b in range(2):
                    ch.pe_prod(pe, i, b, 1)
                for b in range(2):
                    back(i, b, 0)
                for b in range(2):
                    ch.pe_rows(pe, i, b)
                for b in range(2):
                    back(i, b, 1)
            peeled(pe, IT, it)

        @block.scalar
        def _(act):
            def rows(i, b, k, source, ready, func):
                q, nt = 2 * i + b, SUB[b]
                act.wait_ge(ready, q + 1)
                after(act, r_st[k][b], 16 * i)
                nc.scalar.activation(R[k][b][:, 0:nt, :], source, func).then_inc(r_set[k], 1)

            def it(i, k, u):
                last = isinstance(i, int) and i == IT - 1
                for b, nt in enumerate(SUB):
                    ch.act_h0(act, i, b)
                for b, nt in enumerate(SUB):
                    rows(i, b, 0, ch.NR[b][:, 0:nt, :], ch.ln1.normed, AF.Relu)
                for b, nt in enumerate(SUB):
                    ch.act_h(act, i, b, 0, read=turned[0])
                if not last:
                    for b, nt in enumerate(SUB):
                        ch.ln1.act_std(act, 2 * i + 2 + b, b, nt)
                for b, nt in enumerate(SUB):
                    ch.act_h(act, i, b, 1, read=turned[1])
                for b, nt in enumerate(SUB):
                    rows(i, b, 1, PR[b][:, 0:nt * P], turned[0], AF.Copy)
                for b, nt in enumerate(SUB):
                    ch.ln2.act_std(act, 2 * i + b, b, nt)
                for b in range(2):
                    ch.act_hin(act, i, b)
            for b, nt in enumerate(SUB):
                ch.ln1.act_std(act, b, b, nt)
            peeled2x(act, IT, it)

        @block.sync
        def _(sp):
            def it(i):
                def st(b, table, base, rows, ready, done):
                    sp.wait_ge(ready, 2 * i + b + 1)
                    sp.dma_start(edge_rows(table, base, first_tile(i, b), SUB[b]), rows[:, 0:SUB[b], :]).then_inc(done, 16)
                for k in range(2):
                    for b in range(2):
                        st(b, msg_tab[k], 0, R[k][b], r_set[k], r_st[k][b])
                for b in range(2):
                    st(b, x1_tab, E0, ch.X1[b], ch.x1, ch.x1_st[b])
                for b in range(2):
                    st(b, msg_tab[2], 0, R[2][b], r_set[2], r_st[2][b])
                for b in range(2):
                    sp.wait_ge(ch.hin, 2 * i + b + 1)
                    for table, base in ((msg_tab[3], 0), (hin_tab, E0)):
                        sp.dma_start(edge_rows(table, base, first_tile(i, b), SUB[b]), ch.HI[b][:, 0:SUB[b], 0:D]).then_inc(ch.hin_st[b], 16)
            peeled(sp, IT, it)
            for b in range(2):
                sp.wait_ge(ch.hin_st[b], 32 * IT)
                for s in [ch.x1_st[b]] + [r_st[k][b] for k in range(3)]:
                    sp.wait_ge(s, 16 * IT)
    end(ctx)

    G = [sb(top, f"h_G{b}", [P, 4, D]) for b in range(2)]
    M = [sb(top, f"h_M{b}", [P, 4, D]) for b in range(2)]
    T = [sb(top, f"h_T{b}", [P, 4 * P]) for b in range(2)]
    Z = [sb(top, f"h_Z{b}", [P, 4, D]) for b in range(2)]
    hix = [sb(top, f"h_ix{b}", [P, 4], I32) for b in range(2)]
    PH = [ps(top, f"h_P{b}") for b in range(2)]
    h_ix, h_got, h_msg, h_turn = sem("h_ix"), sems("h_got", 2), sem("h_msg"), sem("h_turn")
    h_sum, h_prod, h_z, h_out = sem("h_sum"), sem("h_prod"), sem("h_z"), sem("h_out")
    h_ld, h_st, h_mid = sems("h_ld", 2), sems("h_st", 2), sem("h_mid")
    HN = 2 * IT
    PLAIN = 4

    class Hop:

        def __init__(self, h, kind, table, W=None, scale=None, bias=None, store=None):
            self.h, self.kind, self.table, self.W, self.scale, self.bias, self.store = h, kind, table, W, scale, bias, store
            self.skipped = STEPS * HN if kind == "last" else 0

        def at(self, i, b):
            return self.h * HN + 2 * i + b, self.h * IT + i, first_tile(i, b), SUB[b]

        def pool_gather(self, pool, i, b):
            n, use, t, nt = self.at(i, b)
            if self.kind == "walk":
                pool.wait_ge(h_turn, n - 1)
            else:
                after(pool, h_msg, n - self.skipped - 1)
            nc.gpsimd.tensor_copy(hix[b][:, 0:nt], row_i[:, bass.ds(t, nt)]).then_inc(h_ix, 1)
            wait_apart(pool, (h_ix, n + 1))
            for j in range(nt):
                pool.indirect_dma_start(out=G[b][:, j, :], out_offset=None, in_=self.table[:, :],
                                        in_offset=bass.IndirectOffsetOnAxis(ap=hix[b][:, j:j + 1], axis=0)).then_inc(h_got[b], 16)

        def dve_messages(self, dve, i, b, features=None, features_in=None):
            n, use, t, nt = self.at(i, b)
            dve.wait_ge(h_got[b], (use + 1) * (16 * nt))
            after(dve, h_turn, n - 1)
            if self.kind == "gcn":
                for j in range(nt):
                    last = nc.vector.scalar_tensor_tensor(M[b][:, j, :], G[b][:, j, :], wE[:, bass.ds(t + j, 1)],
                                                          RS[:, bass.ds(t + j, 1), :].rearrange("p o d -> p (o d)"), ALU.mult, ALU.add)
            elif self.kind == "mean":
                dve.wait_ge(features_in[b], 16 * (i + 1))
                nc.vector.tensor_tensor(Z[b][:, 0:nt, :], G[b][:, 0:nt, :], features[b][:, 0:nt, :], ALU.add).then_inc(h_mid, 1)
                dve.wait_ge(h_mid, 2 * i + b + 1)
                last = nc.vector.tensor_tensor(M[b][:, 0:nt, :], Z[b][:, 0:nt, :], RS[:, bass.ds(t, nt), :], ALU.add)
            else:
                last = nc.vector.tensor_tensor(M[b][:, 0:nt, :], G[b][:, 0:nt, :], RS[:, bass.ds(t, nt), :], ALU.add)
            last.then_inc(h_msg, 1)

        def pe_turn(self, pe, i, b):
            n, use, t, nt = self.at(i, b)
            rows = M
            if self.kind == "walk":
                rows = G
                pe.wait_ge(h_got[b], (use + 1) * (16 * nt))
            else:
                pe.wait_ge(h_msg, n - self.skipped + 1)
            after(pe, h_z, n - 1)
            for j in range(nt):
                last = nc.tensor.transpose(PH[b][:, j * P:(j + 1) * P], rows[b][:, j, :], ident[:, :])
            last.then_inc(h_turn, 1)

        def dve_sum(self, dve, i, b):
            n, use, t, nt = self.at(i, b)
            dve.wait_ge(h_turn, n + 1)
            after(dve, h_sum, n)
            after(dve, h_prod, n - 1)
            w = SUB[1 - b] * P
            nc.vector.tensor_tensor_scan(T[b][:, 0:nt * P], keep[:, bass.ds(t * P, nt * P)], PH[b][:, 0:nt * P],
                                         T[1 - b][:, w - 1:w], ALU.mult, ALU.add).then_inc(h_sum, 1)

        def pe_prod(self, pe, i, b):
            n, use, t, nt = self.at(i, b)
            pe.wait_ge(h_sum, n + 1)
            for j in range(nt):
                out_t, sums = PH[b][:, j * P:(j + 1) * P], T[b][:, j * P:(j + 1) * P]
                if self.kind == "mean":
                    last = nc.tensor.transpose(out_t, sums, ident[:, :])
                else:
                    last = nc.tensor.matmul(out_t, sums, self.W[:, :], start=True, stop=True)
            last.then_inc(h_prod, 1)

        def dve_affine(self, dve, i, b):
            n, use, t, nt = self.at(i, b)
            dve.wait_ge(h_prod, n + 1)
            after(dve, h_out, n - 1)
            for j in range(nt):
                last = nc.vector.scalar_tensor_tensor(Z[b][:, j, :], PH[b][:, j * P:(j + 1) * P], self.scale[:, bass.ds(t + j, 1)],
                                                      self.bias[:, :], ALU.mult, ALU.add)
            last.then_inc(h_z, 1)

    pg = ExitStack()
    PG = ps(pg, "PG")
    PG_S = 2 * D
    zeros3 = sb(pg, "zeros3", [3, P], BF16)
    zeros3_set = sem("zeros3_set")
    ctx = phase()
    da = Chain(ctx, "a", 4, (4, 4), gram=True)
    xs = [sb(ctx, f"h_xs{b}", [P, 4, D]) for b in range(2)]
    ones_set, xs_in = sem("ones_set"), sems("xs_in", 2)
    hops = [Hop(0, "gcn", msg_tab[0], w01, dinvw, rb01, msg_tab[1]), Hop(1, "gcn", msg_tab[1], w02, dinvw, rb02, msg_tab[2]),
            Hop(2, "gcn", msg_tab[2], w3l, dinvw, rb3l)]
    PAIRS = DG // 2
    PRE = PAIRS - 3 * IT

    def dense_load(eng, table, g, tile, s):
        if isinstance(g, int) and g == DG - 1:
            eng.dma_start(tile[0:TAILP, :, :], table[g * GR:N, :].rearrange("(p j) d -> p j d", j=4)).then_inc(s, 16)
        else:
            eng.dma_start(tile[:, :, :], group_rows(table, g)).then_inc(s, 16)

    def interleaved(eng, step, start=None):
        for j in range(PRE):
            step(None, 0, j // 2, j % 2)
        for hop in hops:
            if start:
                start(hop)

            def two(k):
                for u in range(2):
                    o = PRE + hop.h * IT + u
                    step(hop, 2 * k + u, k + o // 2, o % 2)
            hi = IT // 2 - (2 if hop.h == 2 else 1)
            two(0)
            with eng.Fori(1, hi) as k:
                two(k)
            for k in range(hi, IT // 2):
                two(k)

    with nc.Block() as block:
        @block.sync
        def _(sp):
            for g in range(4):
                dense_load(sp, x, g, da.X[g], da.x_in[g])

            def hin_store(j):
                for b in range(2):
                    sp.wait_ge(da.hin, 2 * j + b + 1)
                    sp.dma_start(group_rows(hin_tab, 2 * j + b), da.HI[b][:, :, 0:D]).then_inc(da.hin_st[b], 16)

            def step(hop, i, jj, s):
                j = 2 * jj + s
                if hop is not None and hop.h == 2:
                    for b, nt in enumerate(SUB):
                        n, use, t, nt = hop.at(i, b)
                        sp.wait_ge(h_out, n - 1)
                        sp.dma_start(xs[b][:, 0:nt, :], edge_rows(x_s, 0, t, nt)).then_inc(xs_in[b], 16)
                if not (isinstance(j, int) and j == 0):
                    hin_store(j - 1)
                for b in range(2):
                    sp.wait_ge(da.x1, 2 * j + b + 1)
                    if not (isinstance(j, int) and j + 2 >= PAIRS):
                        dense_load(sp, x, 2 * (j + 2) + b, da.X[2 * s + b], da.x_in[2 * s + b])
                    sp.dma_start(group_rows(x1_tab, 2 * j + b), da.X1[b][:, :, :]).then_inc(da.x1_st[b], 16)
                if hop is not None and hop.h < 2:
                    for b in range(2):
                        n, use, t, nt = hop.at(i, b)
                        sp.wait_ge(h_out, n + 1)
                        sp.dma_start(edge_rows(hop.store, RR, t, nt), RS[:, bass.ds(t, nt), :]).then_inc(h_st[b], 16)
            interleaved(sp, step)
            hin_store(PAIRS - 1)
            for b in range(2):
                sp.wait_ge(da.x1_st[b], 16 * PAIRS)
                sp.wait_ge(da.hin_st[b], 16 * PAIRS)

        @block.gpsimd
        def _(pool):
            nc.gpsimd.memset(zeros3[:, :], 0.0).then_inc(zeros3_set, 1)
            for b in range(2):
                nc.gpsimd.memset(T[b][:, :], 0.0)
                last = nc.gpsimd.memset(da.HI[b][:, :, D:D + 1], 1.0)
            last.then_inc(ones_set, 1)
            def start(hop):
                for b in range(2):
                    after(pool, h_st[b], 16 * IT * hop.h)

            def step(hop, i, jj, s):
                if hop is not None:
                    for b in range(2):
                        hop.pool_gather(pool, i, b)
            interleaved(pool, step, start)

        @block.vector
        def _(dve):
            def ln1_apply(j, s):
                for b in range(2):
                    da.ln1.dve_rstd(dve, 2 * j + b, b, 4)
                    after(dve, da.t0, 2 * j + b - 1)
                    da.ln1.dve_apply(dve, 2 * j + b, b, 4, da.X[2 * s + b], da.NR[b])

            def ln2_rstd(j):
                for b in range(2):
                    da.ln2.dve_rstd(dve, 2 * j + b, b, 4, mask=maskd[:, bass.ds(2 * j + b, 1), :].rearrange("p o j -> p (o j)"))

            dve.wait_ge(ones_set, 1)
            for b in range(2):
                dve.wait_ge(da.x_in[b], 16)
                da.ln1.dve_moments(dve, b, b, 4, da.X[b])
            ln1_apply(0, 0)

            def step(hop, i, jj, s):
                j = 2 * jj + s
                s1, uses = 1 - s, jj + s + 1
                more = not (isinstance(j, int) and j + 1 >= PAIRS)
                if hop is not None:
                    for b in range(2):
                        hop.dve_messages(dve, i, b)
                if not (isinstance(j, int) and j == 0):
                    ln2_rstd(j - 1)
                if more:
                    for b in range(2):
                        dve.wait_ge(da.x_in[2 * s1 + b], 16 * uses)
                        da.ln1.dve_moments(dve, 2 * j + 2 + b, b, 4, da.X[2 * s1 + b])
                if hop is not None:
                    for b in range(2):
                        hop.dve_sum(dve, i, b)
                if more:
                    ln1_apply(j + 1, s1)
                if hop is not None:
                    for b in range(2):
                        hop.dve_affine(dve, i, b)
                for b in range(2):
                    da.dve_x1(dve, j, b, s)
                if hop is not None and hop.h == 2:
                    for b in range(2):
                        n, use, t, nt = hop.at(i, b)
                        dve.wait_ge(xs_in[b], 16 * (i + 1))
                        dve.wait_ge(h_z, n + 1)
                        nc.vector.tensor_tensor(RS[:, bass.ds(t, nt), :], Z[b][:, 0:nt, :], xs[b][:, 0:nt, :], ALU.add).then_inc(h_out, 1)
            interleaved(dve, step)
            ln2_rstd(PAIRS - 1)

        @block.tensor
        def _(pe):
            pe.wait_ge(zeros3_set, 1)
            nc.tensor.matmul(PG[:, 0:PG_S + D + 1], zeros3[:, :], split_x1[:, 0:PG_S + D + 1], start=True, stop=False)

            def add_gram(j):
                for b in range(2):
                    pe.wait_ge(da.hin, 2 * j + b + 1)
                    for k in range(4):
                        last = nc.tensor.matmul(PG[:, 0:D + 1], da.HI[b][:, k, 0:D], da.HI[b][:, k, 0:D + 1], start=False, stop=False,
                                                skip_group_check=True)
                    last.then_inc(da.gr, 1)

            def step(hop, i, jj, s):
                j = 2 * jj + s
                for b in range(2):
                    da.pe_turn(pe, j, b)
                if hop is not None:
                    for b in range(2):
                        hop.pe_turn(pe, i, b)
                for b in range(2):
                    da.pe_prod(pe, j, b, 0)
                for b in range(2):
                    da.pe_prod(pe, j, b, 1)
                if hop is not None:
                    for b in range(2):
                        hop.pe_prod(pe, i, b)
                for b in range(2):
                    da.pe_rows(pe, j, b)
                if not (isinstance(j, int) and j == 0):
                    add_gram(j - 1)
            interleaved(pe, step)
            add_gram(PAIRS - 1)

        @block.scalar
        def _(act):
            def hin(j):
                for b in range(2):
                    da.ln2.act_std(act, 2 * j + b, b, 4)
                for b in range(2):
                    da.act_hin(act, j, b)
            for b in range(2):
                da.ln1.act_std(act, b, b, 4)

            def step(hop, i, jj, s):
                j = 2 * jj + s
                for b in range(2):
                    da.act_h0(act, j, b)
                if not (isinstance(j, int) and j == 0):
                    hin(j - 1)
                for b in range(2):
                    da.act_h(act, j, b, 0)
                if not (isinstance(j, int) and j + 1 >= PAIRS):
                    for b in range(2):
                        da.ln1.act_std(act, 2 * j + 2 + b, b, 4)
                for b in range(2):
                    da.act_h(act, j, b, 1)
                if hop is not None and hop.h < 2:
                    for b in range(2):
                        n, use, t, nt = hop.at(i, b)
                        act.wait_ge(h_z, n + 1)
                        for k in range(nt):
                            last = nc.scalar.activation(RS[:, bass.ds(t + k, 1), :], Z[b][:, k:k + 1, :], AF.Relu,
                                                        scale=uw[:, bass.ds(t + k, 1)])
                        last.then_inc(h_out, 1)
            interleaved(act, step)
            hin(PAIRS - 1)
    end(ctx)

    ctx = phase()
    HR = [sb(ctx, f"m_H{b}", [P, 4, D]) for b in range(2)]
    ln = Norm(ctx, "m_ln", on_act=True)
    m_x1_st, m_h_st, m_h, m_v = sems("m_x1_st", 2), sems("m_h_st", 2), ln.normed, sem("m_v")
    with nc.Block() as block:
        @block.sync
        def _(sp):
            def it(i):
                for b, nt in enumerate(SUB):
                    t = first_tile(i, b)
                    after(sp, m_v, 2 * i + b - 1)
                    sp.dma_start(edge_rows(x1_tab, S0, t, nt), RS[:, bass.ds(t, nt), :]).then_inc(m_x1_st[b], 16)
                for b, nt in enumerate(SUB):
                    sp.wait_ge(m_h, 2 * i + b + 1)
                    sp.dma_start(edge_rows(msg_tab[3], RR, first_tile(i, b), nt), HR[b][:, 0:nt, :]).then_inc(m_h_st[b], 16)
            peeled(sp, IT, it)
            for b in range(2):
                sp.wait_ge(m_x1_st[b], 16 * IT)
                sp.wait_ge(m_h_st[b], 16 * IT)

        @block.vector
        def _(dve):
            def moments(i):
                for b, nt in enumerate(SUB):
                    ln.dve_moments(dve, 2 * i + b, b, nt, _Rows(RS, first_tile(i, b)))

            def rstd(i):
                for b, nt in enumerate(SUB):
                    ln.dve_rstd(dve, 2 * i + b, b, nt, mask=isend[:, bass.ds(first_tile(i, b), nt)])

            def scaled(i):
                for b, nt in enumerate(SUB):
                    q, t = 2 * i + b, first_tile(i, b)
                    dve.wait_ge(m_h, q + 1)
                    dve.wait_ge(m_x1_st[b], 16 * (i + 1))
                    for j in range(nt):
                        last = nc.vector.tensor_scalar(RS[:, bass.ds(t + j, 1), :], HR[b][:, j:j + 1, :],
                                                       vscale[:, bass.ds(t + j, 1)], None, ALU.mult)
                    last.then_inc(m_v, 1)
            moments(0)
            rstd(0)
            with dve.Fori(1, IT) as i:
                moments(i)
                scaled(i - 1)
                rstd(i)
            scaled(IT - 1)

        @block.scalar
        def _(act):
            def it(i):
                for b, nt in enumerate(SUB):
                    ln.act_std(act, 2 * i + b, b, nt)
                for b, nt in enumerate(SUB):
                    q = 2 * i + b
                    after(act, m_v, q - 1)
                    after(act, m_h_st[b], 16 * i)
                    ln.act_apply(act, q, b, nt, _Rows(RS, first_tile(i, b)), HR[b])
            peeled(act, IT, it)
    end(ctx)

    ctx = phase()
    FE = [sb(ctx, f"m_F{b}", [P, 4, D]) for b in range(2)]
    MH = [sb(ctx, f"m_M{b}", [P, 4, 130]) for b in range(2)]
    feat_in, feat_pad, mh_st, mh_ones = sems("feat_in", 2), sem("feat_pad"), sems("mh_st", 2), sem("mh_ones")
    mean = Hop(3, "mean", msg_tab[3])
    n0 = mean.h * HN
    with nc.Block() as block:
        @block.sync
        def _(sp):
            def load(i):
                for b, nt in enumerate(SUB):
                    n, use, t, nt = mean.at(i, b)
                    sp.wait_ge(h_msg, n - 1)
                    if isinstance(i, int) and i == IT - 1 and b == 1:
                        sp.dma_start(FE[b][:, 0:nt - 1, :], edge_rows(attr, 0, t, nt - 1)).then_inc(feat_pad, 16)
                        sp.wait_ge(feat_pad, 16)
                        sp.dma_start(FE[b][0:REST, nt - 1, :], attr[FULL * P:E, :]).then_inc(feat_in[b], 16)
                    else:
                        sp.dma_start(FE[b][:, 0:nt, :], edge_rows(attr, 0, t, nt)).then_inc(feat_in[b], 16)

            def store(i):
                for b, nt in enumerate(SUB):
                    n, use, t, nt = mean.at(i, b)
                    sp.wait_ge(h_z, n + 1)
                    sp.dma_start(edge_rows(hin_tab, S0, t, nt), MH[b][:, 0:nt, 0:D]).then_inc(mh_st[b], 16)
            load(0)
            with sp.Fori(0, IT - 2) as i:
                load(i + 1)
                store(i)
            load(IT - 1)
            store(IT - 2)
            store(IT - 1)
            for b in range(2):
                sp.wait_ge(mh_st[b], 16 * IT)

        @block.gpsimd
        def _(pool):
            for b in range(2):
                last = nc.gpsimd.memset(MH[b][:, :, D:D + 1], 1.0)
            last.then_inc(mh_ones, 1)
            with pool.Fori(0, IT) as i:
                for b in range(2):
                    mean.pool_gather(pool, i, b)

        @block.vector
        def _(dve):
            with dve.Fori(0, IT) as i:
                for b in range(2):
                    mean.dve_messages(dve, i, b, FE, feat_in)
                for b in range(2):
                    mean.dve_sum(dve, i, b)

        @block.tensor
        def _(pe):
            pe.wait_ge(mh_ones, 1)

            def add_gram(i):
                for b, nt in enumerate(SUB):
                    pe.wait_ge(h_z, n0 + 2 * i + b + 1)
                    for k in range(nt):
                        last = nc.tensor.matmul(PG[:, PG_S:PG_S + D + 1], MH[b][:, k, 0:D], MH[b][:, k, 0:D + 1], start=False, stop=False,
                                                skip_group_check=True)
                    last.then_inc(h_out, 1)

            def it(i):
                for b in range(2):
                    mean.pe_turn(pe, i, b)
                if not isinstance(i, int):
                    add_gram(i - 1)
                for b in range(2):
                    mean.pe_prod(pe, i, b)
            peeled(pe, IT, it)
            add_gram(IT - 1)
            nc.tensor.matmul(PG[:, 0:PG_S + D + 1], zeros3[:, :], split_x1[:, 0:PG_S + D + 1], start=False, stop=True)

        @block.scalar
        def _(act):
            def it(i):
                for b, nt in enumerate(SUB):
                    n, use, t, nt = mean.at(i, b)
                    act.wait_ge(h_prod, n + 1)
                    after(act, mh_st[b], 16 * i)
                    act.wait_ge(h_out, n - 1)
                    for k in range(nt):
                        last = nc.scalar.activation(MH[b][:, k, 0:D], PH[b][:, k * P:(k + 1) * P], AF.Identity,
                                                    scale=inv_end[:, bass.ds(t + k, 1)])
                    last.then_inc(h_z, 1)
            peeled(act, IT, it)
    end(ctx)

    ctx = phase()
    q1 = sb(ctx, "b_q1", [P, 2 * D])
    gram2 = sb(ctx, "b_gram2", [P, PG_S + D + 1])
    w11e = sb(ctx, "b_w11e", [P, 2 * D])
    onec = sb(ctx, "b_onec", [P, 1])
    c2 = [sb(ctx, f"b_c{k}", [P, 2]) for k in range(8)]
    rec = sb(ctx, "b_rec", [P, GROUPS, 6])
    ag = sb(ctx, "b_ag", [P, 2])
    y0 = sb(ctx, "b_y0", [P, 1])
    c1 = [sb(ctx, f"b_d{k}", [P, 1]) for k in range(8)]
    g_cp, g_pe, g_dve, g_pool = sem("g_cp"), sem("g_pe"), sem("g_dve"), sem("g_pool")
    bn_own, bn2_own = sem("bn_own"), sem("bn2_own")
    pool_pow = sem("pool_pow")
    PB1 = ps(ctx, "b_P1")
    with nc.Block() as block:
        @block.scalar
        def _(act):
            nc.scalar.activation(gram2[:, :], PG[:, 0:PG_S + D + 1], AF.Copy, scale=1.0 / N).then_inc(g_cp, 1)

        @block.gpsimd
        def _(pool):
            nc.gpsimd.memset(onec[:, :], 1.0).then_inc(g_pool, 1)
            pool.wait_ge(g_dve, 2)
            nc.gpsimd.tensor_tensor(c2[2][:, :], c2[1][:, :], neghalf[:, 0:2], ALU.pow).then_inc(pool_pow, 1)

        @block.tensor
        def _(pe):
            pe.wait_ge(g_cp, 2)
            pe.wait_ge(g_pool, 1)
            nc.tensor.matmul(PB1[:, 0:2 * D], gram[:, 0:D], w11[:, :], start=True, stop=True).then_inc(g_pe, 1)
            pe.wait_ge(g_dve, 1)
            for c in range(2):
                nc.tensor.matmul(PB1[:, c:c + 1], q1[:, c * D:(c + 1) * D], onec[:, :], start=True, stop=True)
                last = nc.tensor.matmul(PB1[:, 2 + c:3 + c], w11[:, c * D:(c + 1) * D], gram[:, D:D + 1], start=True, stop=True)
            last.then_inc(g_pe, 1)
            pe.wait_ge(g_dve, 3)
            for c in range(2):
                last = nc.tensor.matmul(PB1[:, 4:5], w12[:, c, :], c2[5][:, c:c + 1], start=(c == 0), stop=(c == 1))
            last.then_inc(g_pe, 1)

        @block.vector
        def _(dve):
            own = [0]

            def step(ins):
                own[0] += 1
                ins.then_inc(bn_own, 1)
                dve.wait_ge(bn_own, own[0])

            step(nc.vector.tensor_scalar(w11e[:, :], w11[:, :], epsc[:, 1:2], None, ALU.mult))
            step(nc.vector.tensor_tensor(ag[:, 0:1], epsc[:, 1:2], epsc[:, 1:2], ALU.mult))
            dve.wait_ge(g_cp, 1)
            nc.vector.scalar_tensor_tensor(gram[:, 0:D], gram2[:, 0:D], ag[:, 0:1], gram2[:, PG_S:PG_S + D], ALU.mult, ALU.add)
            nc.vector.scalar_tensor_tensor(gram[:, D:D + 1], gram2[:, D:D + 1], epsc[:, 1:2], gram2[:, PG_S + D:PG_S + D + 1],
                                           ALU.mult, ALU.add).then_inc(g_cp, 1)
            dve.wait_ge(g_pe, 1)
            nc.vector.tensor_tensor(q1[:, :], w11[:, :], PB1[:, 0:2 * D], ALU.mult).then_inc(g_dve, 1)
            dve.wait_ge(g_pe, 2)
            step(nc.vector.tensor_copy(c2[0][:, :], PB1[:, 2:4]))
            step(nc.vector.tensor_tensor(c2[1][:, :], c2[0][:, :], c2[0][:, :], ALU.mult))
            step(nc.vector.tensor_tensor(c2[1][:, :], PB1[:, 0:2], c2[1][:, :], ALU.subtract))
            nc.vector.tensor_scalar(c2[1][:, :], c2[1][:, :], 0.0, BN_EPS, ALU.max, ALU.add).then_inc(g_dve, 1)
            dve.wait_ge(pool_pow, 1)
            step(nc.vector.tensor_tensor(bn1[:, 0:2], c2[2][:, :], col[:, C_GA1:C_GA1 + 2], ALU.mult))
            step(nc.vector.tensor_tensor(c2[3][:, :], c2[0][:, :], col[:, C_B11:C_B11 + 2], ALU.add))
            step(nc.vector.tensor_tensor(c2[3][:, :], col[:, C_B11:C_B11 + 2], c2[3][:, :], ALU.subtract))
            step(nc.vector.tensor_tensor(c2[4][:, :], c2[3][:, :], bn1[:, 0:2], ALU.mult))
            step(nc.vector.tensor_tensor(bn1[:, 2:4], c2[4][:, :], col[:, C_BE1:C_BE1 + 2], ALU.add))
            nc.vector.tensor_scalar(c2[5][:, :], bn1[:, 2:4], 0.0, None, ALU.max).then_inc(g_dve, 1)
            dve.wait_ge(g_pe, 3)
            step(nc.vector.tensor_tensor(y0[:, :], PB1[:, 4:5], col[:, C_B12:C_B12 + 1], ALU.add))

    ctx2 = phase()
    HI = [sb(ctx2, f"b_HI{b}", [P, 4, D]) for b in range(2)]
    HT = [sb(ctx2, f"b_HT{b}", [P, 512]) for b in range(2)]
    ZT = [[sb(ctx2, f"b_Z{c}{b}", [P, 512]) for b in range(2)] for c in range(2)]
    Y = [sb(ctx2, f"b_Y{b}", [P, 512]) for b in range(2)]
    BP = [ps(ctx2, f"b_BP{b}") for b in range(2)]
    BQ = [ps(ctx2, f"b_BQ{b}") for b in range(2)]
    b_in, b_turn, b_ht, b_p1, b_z, b_p2, b_y, b_rec, b_st = (sems("b_in", 2), sem("b_turn"), sem("b_ht"), sems("b_p1_", 2),
                                                            sems("b_z_", 2), sem("b_p2"), sem("b_y"), sem("b_rec"), sems("b_st", 2))
    BPAIRS = GROUPS // 2
    with nc.Block() as block:
        @block.sync
        def _(sp):
            for b in range(2):
                sp.dma_start(HI[b][:, :, :], group_rows(hin_tab, b)).then_inc(b_in[b], 16)

            def it(j):
                for b in range(2):
                    if not (isinstance(j, int) and j == BPAIRS - 1):
                        sp.wait_ge(b_turn, 2 * j + b + 1)
                        sp.dma_start(HI[b][:, :, :], group_rows(hin_tab, 2 * j + 2 + b)).then_inc(b_in[b], 16)
                for b in range(2):
                    sp.wait_ge(b_y, 2 * j + b + 1)
                    sp.dma_start(y2_tab[bass.ds(2 * j + b, 1), :, :].rearrange("o p r -> p (o r)"), Y[b][:, :]).then_inc(b_st[b], 16)
            with sp.Fori(0, BPAIRS - 1) as j:
                it(j)
            it(BPAIRS - 1)
            for b in range(2):
                sp.wait_ge(b_st[b], 16 * BPAIRS)

        @block.tensor
        def _(pe):
            def turn(j):
                for b in range(2):
                    q = 2 * j + b
                    pe.wait_ge(b_in[b], 16 * (j + 1))
                    after(pe, b_y, q - 1)
                    for k in range(4):
                        last = nc.tensor.transpose(BP[b][:, k * P:(k + 1) * P], HI[b][:, k, :], ident[:, :])
                    last.then_inc(b_turn, 1)

            def it(j, w1):
                turn(j)
                for c in range(2):
                    for b in range(2):
                        q = 2 * j + b
                        pe.wait_ge(b_ht, q + 1)
                        if c:
                            pe.wait_ge(b_z[0], q + 1)
                        else:
                            after(pe, b_z[1], q - 1)
                        nc.tensor.matmul(BQ[b][:, :], w1[b][:, c * D:(c + 1) * D], HT[b][:, :], start=True, stop=True).then_inc(b_p1[c], 1)
                for b in range(2):
                    q = 2 * j + b
                    for c in range(2):
                        pe.wait_ge(b_z[c], q + 1)
                        last = nc.tensor.matmul(BP[b][:, :], w12[:, c, :], ZT[c][b][:, :], start=(c == 0), stop=(c == 1))
                    last.then_inc(b_p2, 1)
            FIRST_S = DG + RG
            assert FIRST_S % 2
            it(0, (w11e, w11e))
            with pe.Fori(1, FIRST_S // 2) as j:
                it(j, (w11e, w11e))
            it(FIRST_S // 2, (w11e, w11))
            with pe.Fori(FIRST_S // 2 + 1, BPAIRS) as j:
                it(j, (w11, w11))

        @block.scalar
        def _(act):
            def it(j):
                for b in range(2):
                    q = 2 * j + b
                    act.wait_ge(b_turn, q + 1)
                    after(act, b_p1[1], q - 1)
                    nc.scalar.activation(HT[b][:, :], BP[b][:, :], AF.Copy).then_inc(b_ht, 1)
                for c in range(2):
                    for b in range(2):
                        q = 2 * j + b
                        act.wait_ge(b_p1[c], q + 1)
                        after(act, b_p2, q - 1)
                        nc.scalar.activation(ZT[c][b][:, :], BQ[b][:, :], AF.Relu, bias=bn1[:, 2 + c:3 + c],
                                             scale=bn1[:, c:c + 1]).then_inc(b_z[c], 1)
            peeled(act, BPAIRS, it)

        @block.vector
        def _(dve):
            def it(j):
                for b in range(2):
                    q = 2 * j + b
                    dve.wait_ge(b_p2, q + 1)
                    after(dve, b_st[b], 16 * j)
                    after(dve, b_rec, q - 1)
                    nc.vector.tensor_scalar(Y[b][:, :], BP[b][:, :], col[:, C_B12:C_B12 + 1], None, ALU.add).then_inc(b_y, 1)
                    dve.wait_ge(b_y, q + 1)
                    nc.vector.bn_stats(rec[:, bass.ds(q, 1), :].rearrange("p o s -> p (o s)"), Y[b][:, :]).then_inc(b_rec, 1)
            peeled(dve, BPAIRS, it)
    end(ctx2)

    with nc.Block() as block:
        @block.vector
        def _(dve):
            own = [0]

            def step(ins):
                own[0] += 1
                ins.then_inc(bn2_own, 1)
                dve.wait_ge(bn2_own, own[0])

            ALLR = float((DG + RG) * GR)
            step(nc.vector.tensor_copy(rec[:, DG:DG + RG, :], rec[:, DG + RG:GROUPS, :]))
            step(nc.vector.bn_aggr(ag[:, :], rec[:, 0:DG + RG, :].rearrange("p g s -> p (g s)")))
            step(nc.vector.tensor_tensor(c1[0][:, :], ag[:, 0:1], y0[:, :], ALU.subtract))
            step(nc.vector.tensor_scalar(c1[1][:, :], c1[0][:, :], CONST_ROWS / N, None, ALU.mult))
            step(nc.vector.tensor_tensor(c1[2][:, :], ag[:, 0:1], c1[1][:, :], ALU.add))
            step(nc.vector.tensor_tensor(c1[3][:, :], c1[1][:, :], c1[1][:, :], ALU.mult))
            step(nc.vector.tensor_tensor(c1[3][:, :], c1[3][:, :], ag[:, 1:2], ALU.add))
            step(nc.vector.tensor_scalar(c1[3][:, :], c1[3][:, :], ALLR / N, None, ALU.mult))
            step(nc.vector.tensor_tensor(c1[4][:, :], y0[:, :], c1[2][:, :], ALU.subtract))
            step(nc.vector.tensor_tensor(c1[4][:, :], c1[4][:, :], c1[4][:, :], ALU.mult))
            step(nc.vector.tensor_scalar(c1[4][:, :], c1[4][:, :], CONST_ROWS / N, None, ALU.mult))
            step(nc.vector.tensor_tensor(c1[5][:, :], c1[3][:, :], c1[4][:, :], ALU.subtract))
            nc.vector.tensor_scalar(c1[5][:, :], c1[5][:, :], 0.0, BN_EPS, ALU.max, ALU.add).then_inc(g_dve, 1)
            dve.wait_ge(pool_pow, 2)
            step(nc.vector.tensor_tensor(bn2[:, 0:1], c1[6][:, :], col[:, C_GA2:C_GA2 + 1], ALU.mult))
            step(nc.vector.tensor_tensor(c1[7][:, :], c1[2][:, :], bn2[:, 0:1], ALU.mult))
            step(nc.vector.tensor_tensor(bn2[:, 1:2], col[:, C_BE2:C_BE2 + 1], c1[7][:, :], ALU.subtract))

        @block.gpsimd
        def _(pool):
            pool.wait_ge(g_dve, 4)
            nc.gpsimd.tensor_tensor(c1[6][:, :], c1[5][:, :], neghalf[:, 0:1], ALU.pow).then_inc(pool_pow, 1)
    end(ctx)
    pg.close()

    class Late:
        def __init__(self, ctx, tag, full):
            two = lambda n: [sb(ctx, f"{tag}_{n}{b}", [P, 4, D]) for b in range(2)]
            self.Y, self.X1, self.X2, self.ZT = two("Y"), two("X1"), two("X2"), two("ZT")
            self.PT = [ps(ctx, f"{tag}_PT{b}") for b in range(2)]
            self.ln1 = Norm(ctx, f"{tag}_ln1", on_act=True)
            self.y_in, self.x1_in = sems(f"{tag}_y_in", 2), sems(f"{tag}_x1_in", 2)
            self.z, self.turned, self.x2 = sem(f"{tag}_z"), sem(f"{tag}_turned"), sem(f"{tag}_x2")
            if full:
                self.PC = [ps(ctx, f"{tag}_PC{b}") for b in range(2)]
                self.X3, self.HT, self.O, self.NR = two("X3"), two("HT"), two("O"), two("NR")
                self.N2 = self.NR
                self.ln2 = Norm(ctx, f"{tag}_ln2", on_act=True)
                self.x3a, self.x3, self.turned2, self.h, self.p1, self.tanh, self.p2, self.o = (
                    sem(f"{tag}_{n}") for n in ("x3a", "x3", "turned2", "h", "p1", "tanh", "p2", "o"))
                self.o_st = sems(f"{tag}_o_st", 2)

        def load(self, sp, j, g0, b):
            g = g0 + 2 * j + b
            sp.dma_start(self.Y[b][:, :, :].rearrange("p t d -> p (t d)"), y2_tab[bass.ds(g, 1), :, :].rearrange("o p r -> p (o r)")).then_inc(self.y_in[b], 16)
            sp.dma_start(self.X1[b][:, :, :], group_rows(x1_tab, g)).then_inc(self.x1_in[b], 16)

        def act_z(self, act, j, b):
            q = 2 * j + b
            act.wait_ge(self.y_in[b], 16 * (j + 1))
            after(act, self.turned, q - 1)
            nc.scalar.activation(self.ZT[b][:, :, :], self.Y[b][:, :, :], AF.Relu, bias=bn2[:, 1:2], scale=bn2[:, 0:1]).then_inc(self.z, 1)

        def pe_turn(self, pe, j, b):
            q = 2 * j + b
            pe.wait_ge(self.z, q + 1)
            after(pe, self.x2, q - 1)
            for k in range(4):
                last = nc.tensor.transpose(self.PT[b][:, k * P:(k + 1) * P], self.ZT[b][:, k, :], ident[:, :])
            last.then_inc(self.turned, 1)

        def dve_x2(self, dve, j, b):
            q = 2 * j + b
            dve.wait_ge(self.turned, q + 1)
            dve.wait_ge(self.x1_in[b], 16 * (j + 1))
            nc.vector.tensor_tensor(self.X2[b][:, :, :], self.X1[b][:, :, :],
                                    self.PT[b][:, :].rearrange("p (t d) -> p t d", d=D), ALU.add).then_inc(self.x2, 1)
            dve.wait_ge(self.x2, q + 1)
            self.ln1.dve_moments(dve, q, b, 4, self.X2[b])

    ctx = phase()
    es = Late(ctx, "c", False)
    R0 = [sb(ctx, f"c_R{b}", [P, 4, D]) for b in range(2)]
    c_r, c_r_st, c_x2_st = es.ln1.normed, sems("c_r_st", 2), sems("c_x2_st", 2)
    EPAIRS = RG
    with nc.Block() as block:
        @block.sync
        def _(sp):
            for b in range(2):
                es.load(sp, 0, DG, b)

            def it(j):
                for b in range(2):
                    sp.wait_ge(es.x2, 2 * j + b + 1)
                    if not (isinstance(j, int) and j == EPAIRS - 1):
                        es.load(sp, j + 1, DG, b)
                    sp.dma_start(group_rows(x2_tab, 2 * j + b), es.X2[b][:, :, :]).then_inc(c_x2_st[b], 16)
                for b in range(2):
                    sp.wait_ge(c_r, 2 * j + b + 1)
                    sp.dma_start(group_rows(step_tab[0], 2 * j + b), R0[b][:, :, :]).then_inc(c_r_st[b], 16)
            with sp.Fori(0, EPAIRS - 1) as j:
                it(j)
            it(EPAIRS - 1)
            for b in range(2):
                sp.wait_ge(c_x2_st[b], 16 * EPAIRS)
                sp.wait_ge(c_r_st[b], 16 * EPAIRS)

        @block.scalar
        def _(act):
            def it(j):
                if not (isinstance(j, int) and j == EPAIRS - 1):
                    for b in range(2):
                        es.act_z(act, j + 1, b)
                for b in range(2):
                    es.ln1.act_std(act, 2 * j + b, b, 4)
                for b in range(2):
                    after(act, c_r_st[b], 16 * j)
                    es.ln1.act_apply(act, 2 * j + b, b, 4, es.X2[b], R0[b])
            for b in range(2):
                es.act_z(act, 0, b)
            it(0)
            with act.Fori(1, EPAIRS - 1) as j:
                it(j)
            it(EPAIRS - 1)

        @block.tensor
        def _(pe):
            def it(j):
                for b in range(2):
                    es.pe_turn(pe, j, b)
            peeled(pe, EPAIRS, it)

        @block.vector
        def _(dve):
            def it(j):
                for b in range(2):
                    after(dve, c_x2_st[b], 16 * j)
                    after(dve, c_r, 2 * j + b - 1)
                    es.dve_x2(dve, j, b)
                for b in range(2):
                    es.ln1.dve_rstd(dve, 2 * j + b, b, 4)
            peeled(dve, EPAIRS, it)
    end(ctx)

    lctx = phase()
    dl = Late(lctx, "d", True)
    r6x4 = sb(lctx, "r6x4", [P, 4, D])
    r1x4 = sb(lctx, "r1x4", [P, 4, D])
    rs_in, h_re, h_re_st, bias4 = sem("rs_in"), sem("h_re"), sems("h_re_st", 2), sem("bias4")
    HALF = IT // 2

    def first(j):
        return isinstance(j, int) and j == 0

    def final(j):
        return isinstance(j, int) and j == PAIRS - 1

    def dl_load_next(sp, j):
        if not (isinstance(j, int) and j == PAIRS - 1):
            for b in range(2):
                sp.wait_ge(dl.x2, 2 * j + b + 1)
                dl.load(sp, j + 1, 0, b)

    def dl_store(sp, j):
        for b in range(2):
            sp.wait_ge(dl.o, 2 * j + b + 1)
            if isinstance(j, int) and j == PAIRS - 1 and b == 1:
                sp.dma_start(out[(DG - 1) * GR:N, :].rearrange("(p j) d -> p j d", j=4), dl.O[b][0:TAILP, :, :]).then_inc(dl.o_st[b], 16)
            else:
                sp.dma_start(group_rows(out, 2 * j + b), dl.O[b][:, :, :]).then_inc(dl.o_st[b], 16)

    def dl_dve_x2(dve, j):
        for b in range(2):
            after(dve, dl.x3a, 2 * j + b - 1)
            dl.dve_x2(dve, j, b)

    def dl_dve_x3(dve, j):
        for b in range(2):
            q = 2 * j + b
            dve.wait_ge(dl.ln1.normed, q + 1)
            after(dve, dl.o, q - 1)
            nc.vector.tensor_tensor(dl.NR[b][:, :, :], dl.NR[b][:, :, :], dl.X2[b][:, :, :], ALU.add).then_inc(dl.x3a, 1)
            dve.wait_ge(dl.x3a, q + 1)
            nc.vector.tensor_tensor(dl.X3[b][:, :, :], dl.NR[b][:, :, :], r6x4[:, :, :], ALU.add).then_inc(dl.x3, 1)
            dve.wait_ge(dl.x3, q + 1)
            dl.ln2.dve_moments(dve, q, b, 4, dl.X3[b])

    def dl_dve_rstd(dve, j, which):
        for b in range(2):
            (dl.ln1, dl.ln2)[which].dve_rstd(dve, 2 * j + b, b, 4)

    def dl_act_norm(act, j, which):
        ln, rows = ((dl.ln1, dl.X2), (dl.ln2, dl.X3))[which]
        for b in range(2):
            ln.act_std(act, 2 * j + b, b, 4)
        for b in range(2):
            q = 2 * j + b
            if which:
                act.wait_ge(dl.x3, q + 1)
            else:
                after(act, dl.turned2, q - 1)
            ln.act_apply(act, q, b, 4, rows[b], dl.NR[b])

    def dl_dve_out(dve, j):
        for b in range(2):
            q = 2 * j + b
            dve.wait_ge(dl.p2, q + 1)
            after(dve, dl.o_st[b], 16 * j)
            nc.vector.tensor_tensor(dl.O[b][:, :, :], dl.X3[b][:, :, :],
                                    dl.PC[b][:, :].rearrange("p (t d) -> p t d", d=D), ALU.add).then_inc(dl.o, 1)

    def dl_pe_turn(pe, j):
        for b in range(2):
            dl.pe_turn(pe, j, b)

    def dl_pe_turn2(pe, j):
        for b in range(2):
            q = 2 * j + b
            pe.wait_ge(dl.ln2.normed, q + 1)
            after(pe, dl.o, q - 1)
            for k in range(4):
                last = nc.tensor.transpose(dl.PC[b][:, k * P:(k + 1) * P], dl.N2[b][:, k, :], ident[:, :])
            last.then_inc(dl.turned2, 1)

    def dl_pe_prod(pe, j):
        for b in range(2):
            q = 2 * j + b
            pe.wait_ge(dl.h, q + 1)
            nc.tensor.matmul(dl.PC[b][:, :], w31[:, :], dl.HT[b][:, :, :].rearrange("p t d -> p (t d)"), start=True, stop=True).then_inc(dl.p1, 1)

    def dl_pe_rows(pe, j):
        for b in range(2):
            q = 2 * j + b
            pe.wait_ge(dl.tanh, q + 1)
            nc.tensor.matmul(dl.PC[b][:, :], ones3[:, :], split_out[:, :], start=True, stop=False)
            for k in range(4):
                last = nc.tensor.matmul(dl.PC[b][:, k * P:(k + 1) * P], dl.HT[b][:, k, :], w32[:, :], start=False, stop=(k == 3))
            last.then_inc(dl.p2, 1)

    def dl_pe_end(pe, j):
        dl_pe_turn2(pe, j)
        dl_pe_prod(pe, j)
        dl_pe_rows(pe, j)

    def dl_act_z(act, j):
        for b in range(2):
            dl.act_z(act, j, b)

    def dl_act_h(act, j):
        for b in range(2):
            q = 2 * j + b
            act.wait_ge(dl.turned2, q + 1)
            after(act, dl.p2, q - 1)
            nc.scalar.activation(dl.HT[b][:, :, :], dl.PC[b][:, :], AF.Copy).then_inc(dl.h, 1)

    def dl_act_tanh(act, j):
        for b in range(2):
            act.wait_ge(dl.p1, 2 * j + b + 1)
            nc.scalar.activation(dl.HT[b][:, :, :], dl.PC[b][:, :], AF.Tanh, bias=col[:, C_B31:C_B31 + 1]).then_inc(dl.tanh, 1)

    walks = [Hop(PLAIN + w, "walk", step_tab[w % 2], wht, inv_cnt, rbh, step_tab[1 - w % 2] if w < STEPS - 1 else None)
             for w in range(STEPS)]

    ALONE = PAIRS - STEPS * (HALF + 1)

    def beside(eng, w, step):
        if w == 0:
            for j in range(ALONE):
                step(None, j)
        pair0 = ALONE + w * (HALF + 1)
        step(None, pair0)
        with eng.Fori(0, HALF - 1) as k:
            step(2 * k, k + pair0 + 1)
        step(2 * (HALF - 1), HALF - 1 + pair0 + 1)
    assert ALONE >= 1

    with nc.Block() as block:
        @block.sync
        def _(sp):
            sp.dma_start(RE[:, :, :], step_tab[0][0:EP, :].rearrange("(t p) d -> p t d", p=P)).then_inc(rs_in, 16)
            sp.dma_start(RS[:, :, :], step_tab[0][RR:RR + EP, :].rearrange("(t p) d -> p t d", p=P)).then_inc(rs_in, 16)
            for b in range(2):
                dl.load(sp, 0, 0, b)
            for w, hop in enumerate(walks):
                def step(i, j):
                    dl_load_next(sp, j)
                    for u in range(2):
                        if i is not None and hop.store is not None:
                            for b in range(2):
                                n, use, t, nt = hop.at(i + u, b)
                                sp.wait_ge(h_out, n + 1)
                                sp.dma_start(edge_rows(hop.store, RR, t, nt), RS[:, bass.ds(t, nt), :]).then_inc(h_st[b], 16)
                                sp.wait_ge(h_re, n - PLAIN * HN + 1)
                                sp.dma_start(edge_rows(hop.store, 0, t, nt), RE[:, bass.ds(t, nt), :]).then_inc(h_re_st[b], 16)
                        if u == 0 and not first(j):
                            dl_store(sp, j - 1)
                beside(sp, w, step)
            dl_store(sp, PAIRS - 1)
            for b in range(2):
                sp.wait_ge(dl.o_st[b], 16 * PAIRS)

        @block.gpsimd
        def _(pool):
            for w, hop in enumerate(walks):
                if w:
                    for b in range(2):
                        pool.wait_ge(h_st[b], 16 * IT * (2 + w))
                        pool.wait_ge(h_re_st[b], 16 * IT * w)

                def step(i, j):
                    if i is not None:
                        for u in range(2):
                            for b in range(2):
                                hop.pool_gather(pool, i + u, b)
                beside(pool, w, step)

        @block.vector
        def _(dve):
            for k in range(4):
                nc.vector.tensor_copy(r6x4[:, k, :], r6[:, :])
                last = nc.vector.tensor_copy(r1x4[:, k, :], rmsg[:, :])
            last.then_inc(bias4, 1)
            dve.wait_ge(bias4, 1)
            dve.wait_ge(rs_in, 32)
            for w, hop in enumerate(walks):
                def affine(i):
                    for b in range(2):
                        hop.dve_affine(dve, i, b)

                def update(i):
                    for b in range(2):
                        n, use, t, nt = hop.at(i, b)
                        dve.wait_ge(h_z, n + 1)
                        nc.vector.scalar_tensor_tensor(RS[:, bass.ds(t, nt), :], Z[b][:, 0:nt, :], 0.0, RS[:, bass.ds(t, nt), :],
                                                       ALU.max, ALU.add).then_inc(h_out, 1)
                        nc.vector.tensor_tensor(RE[:, bass.ds(t, nt), :], RE[:, bass.ds(t, nt), :], r1x4[:, 0:nt, :], ALU.add).then_inc(h_re, 1)

                def step(i, j):
                    dl_dve_x2(dve, j)
                    if i is not None:
                        for b in range(2):
                            hop.dve_sum(dve, i, b)
                    dl_dve_rstd(dve, j, 0)
                    if i is not None:
                        affine(i)
                        update(i)
                    if not first(j):
                        dl_dve_out(dve, j - 1)
                    if i is not None:
                        for b in range(2):
                            hop.dve_sum(dve, i + 1, b)
                    dl_dve_x3(dve, j)
                    if i is not None:
                        affine(i + 1)
                    dl_dve_rstd(dve, j, 1)
                    if i is not None:
                        update(i + 1)
                beside(dve, w, step)
            dl_dve_out(dve, PAIRS - 1)

        @block.tensor
        def _(pe):
            for w, hop in enumerate(walks):
                def step(i, j):
                    dl_pe_turn(pe, j)
                    if i is not None:
                        for b in range(2):
                            hop.pe_turn(pe, i, b)
                    if not first(j):
                        dl_pe_turn2(pe, j - 1)
                        dl_pe_prod(pe, j - 1)
                    if i is not None:
                        for b in range(2):
                            hop.pe_prod(pe, i, b)
                    if not first(j):
                        dl_pe_rows(pe, j - 1)
                    if i is not None:
                        for b in range(2):
                            hop.pe_turn(pe, i + 1, b)
                        for b in range(2):
                            hop.pe_prod(pe, i + 1, b)
                beside(pe, w, step)
            dl_pe_end(pe, PAIRS - 1)

        @block.scalar
        def _(act):
            dl_act_z(act, 0)
            for w, hop in enumerate(walks):
                def step(i, j):
                    if not first(j):
                        dl_act_h(act, j - 1)
                        dl_act_tanh(act, j - 1)
                    dl_act_norm(act, j, 0)
                    if not final(j):
                        dl_act_z(act, j + 1)
                    dl_act_norm(act, j, 1)
                beside(act, w, step)
            dl_act_h(act, PAIRS - 1)
            dl_act_tanh(act, PAIRS - 1)

    end(lctx)

    ctx = phase()
    last_hop = Hop(PLAIN + STEPS, "last", last_tab, w31, dinvu, rb31)
    kinds = ("e", "s")
    b32x4 = sb(ctx, "b32x4", [P, 4, D])
    X2 = {k: [sb(ctx, f"p{k}_X2{b}", [P, 4, D]) for b in range(4)] for k in kinds}
    HR, X4 = M, Z
    pn = {k: Norm(ctx, f"p{k}_ln", on_act=True) for k in kinds}
    p_in = {k: sems(f"p{k}_in", 4) for k in kinds}
    p_x3 = {k: sem(f"p{k}_x3") for k in kinds}
    p_h = {k: pn[k].normed for k in kinds}
    p_st = {k: sems(f"p{k}_st", 2) for k in kinds}
    p_x4, p_x4_st, p_bias = sem("p_x4"), sems("p_x4_st", 2), sem("p_bias")
    with nc.Block() as block:
        @block.sync
        def _(sp):
            def it(i, k2, u):
                for b, nt in enumerate(SUB):
                    q, t = 2 * i + b, first_tile(i, b)
                    for k, base in (("e", 0), ("s", RR)):
                        after(sp, p_h[k], q - 3)
                        if k == "s":
                            after(sp, p_x4, q - 3)
                        sp.dma_start(X2[k][2 * u + b][:, 0:nt, :], edge_rows(x2_tab, base, t, nt)).then_inc(p_in[k][2 * u + b], 16)
            peeled2(sp, IT, it)

        @block.gpsimd
        def _(pool):
            def it(i):
                for b, nt in enumerate(SUB):
                    wait_apart(pool, (p_x4, 2 * i + b + 1))
                    pool.dma_start(edge_rows(x3_s, 0, first_tile(i, b), nt), X4[b][:, 0:nt, :]).then_inc(p_x4_st[b], 16)
                for b, nt in enumerate(SUB):
                    t = first_tile(i, b)
                    for k, base, rows in (("e", 0, HR[b][:, 0:nt, :]), ("s", RR, RS[:, bass.ds(t, nt), :])):
                        wait_apart(pool, (p_h[k], 2 * i + b + 1))
                        pool.dma_start(edge_rows(last_tab, base, t, nt), rows).then_inc(p_st[k][b], 16)
            peeled(pool, IT, it)
            for b in range(2):
                pool.wait_ge(p_x4_st[b], 16 * IT)
                for k in kinds:
                    pool.wait_ge(p_st[k][b], 16 * IT)

        @block.vector
        def _(dve):
            for k in range(4):
                last = nc.vector.tensor_copy(b32x4[:, k, :], rb32[:, :])
            last.then_inc(p_bias, 1)
            dve.wait_ge(p_bias, 1)

            def it(i, k2, u):
                for b, nt in enumerate(SUB):
                    q, t, r = 2 * i + b, first_tile(i, b), 2 * u + b
                    for k, R in (("e", RE), ("s", RS)):
                        dve.wait_ge(p_in[k][r], 16 * (k2 + 1))
                        nc.vector.tensor_tensor(X2[k][r][:, 0:nt, :], X2[k][r][:, 0:nt, :], R[:, bass.ds(t, nt), :], ALU.add).then_inc(p_x3[k], 1)
                        dve.wait_ge(p_x3[k], q + 1)
                        pn[k].dve_moments(dve, q, b, nt, X2[k][r])
                for b, nt in enumerate(SUB):
                    after(dve, p_x4_st[b], 16 * i)
                    nc.vector.tensor_tensor(X4[b][:, 0:nt, :], X2["s"][2 * u + b][:, 0:nt, :], b32x4[:, 0:nt, :], ALU.add).then_inc(p_x4, 1)
                for b, nt in enumerate(SUB):
                    for k in kinds:
                        pn[k].dve_rstd(dve, 2 * i + b, b, nt, mask=uu[:, bass.ds(first_tile(i, b), nt)] if k == "s" else None)
            peeled2(dve, IT, it)

        @block.scalar
        def _(act):
            def it(i, k2, u):
                for b, nt in enumerate(SUB):
                    for k in kinds:
                        pn[k].act_std(act, 2 * i + b, b, nt)
                for b, nt in enumerate(SUB):
                    q, t = 2 * i + b, first_tile(i, b)
                    after(act, p_st["e"][b], 16 * i)
                    pn["e"].act_apply(act, q, b, nt, X2["e"][2 * u + b], HR[b])
                    pn["s"].act_apply(act, q, b, nt, X2["s"][2 * u + b], _Rows(RS, t))
            peeled2(act, IT, it)
    end(ctx)

    ctx = phase()
    TH = [sb(ctx, f"f_TH{b}", [P, 4, D]) for b in range(2)]
    TT = [sb(ctx, f"f_TT{b}", [P, 4 * P]) for b in range(2)]
    XR = [sb(ctx, f"f_XR{b}", [P, 4, D]) for b in range(2)]
    OR = [sb(ctx, f"f_OR{b}", [P, 4, D]) for b in range(2)]
    fix = [sb(ctx, f"f_ix{b}", [P, 4], I32) for b in range(2)]
    PF = [ps(ctx, f"f_P{b}") for b in range(2)]
    f_turn, f_tt, f_prod, f_o, f_in, f_ix = sem("f_turn"), sem("f_tt"), sem("f_prod"), sem("f_o"), sems("f_in", 2), sem("f_ix")
    scattered = sems("scattered", 2)
    hop = last_hop

    with nc.Block() as block:
        @block.sync
        def _(sp):
            def it(i):
                for b, nt in enumerate(SUB):
                    after(sp, f_o, 2 * i + b - 1)
                    sp.dma_start(XR[b][:, 0:nt, :], edge_rows(x3_s, 0, first_tile(i, b), nt)).then_inc(f_in[b], 16)
            peeled(sp, IT, it)

        @block.gpsimd
        def _(pool):
            def scatter(i):
                for b, nt in enumerate(SUB):
                    q, t = 2 * i + b, first_tile(i, b)
                    after(pool, scattered[b], 16 * nt * i)
                    nc.gpsimd.tensor_copy(fix[b][:, 0:nt], end_i[:, bass.ds(t, nt)]).then_inc(f_ix, 1)
                    wait_apart(pool, (f_ix, q + 1), (f_o, q + 1))
                    for j in range(nt):
                        pool.indirect_dma_start(out=out[:, :], out_offset=bass.IndirectOffsetOnAxis(ap=fix[b][:, j:j + 1], axis=0),
                                                in_=OR[b][:, j, :], in_offset=None, bounds_check=N - 1,
                                                oob_is_err=False).then_inc(scattered[b], 16)
            for i in range(2):
                for b in range(2):
                    hop.pool_gather(pool, i, b)
            scatter(0)
            with pool.Fori(1, IT - 1) as i:
                for b in range(2):
                    hop.pool_gather(pool, i + 1, b)
                scatter(i)
            scatter(IT - 1)
            for b, nt in enumerate(SUB):
                pool.wait_ge(scattered[b], 16 * nt * IT)

        @block.vector
        def _(dve):
            def it(i):
                for b in range(2):
                    hop.dve_messages(dve, i, b)
                for b in range(2):
                    hop.dve_sum(dve, i, b)
                for b in range(2):
                    hop.dve_affine(dve, i, b)
                for b, nt in enumerate(SUB):
                    dve.wait_ge(f_prod, 2 * i + b + 1)
                    dve.wait_ge(f_in[b], 16 * (i + 1))
                    after(dve, scattered[b], 16 * nt * i)
                    nc.vector.tensor_tensor(OR[b][:, 0:nt, :], XR[b][:, 0:nt, :],
                                            PF[b][:, 0:nt * P].rearrange("p (t d) -> p t d", d=D), ALU.add).then_inc(f_o, 1)
            peeled(dve, IT, it)

        @block.tensor
        def _(pe):
            def it(i):
                for b in range(2):
                    hop.pe_turn(pe, i, b)
                for b in range(2):
                    hop.pe_prod(pe, i, b)
                for b, nt in enumerate(SUB):
                    n, use, t, nt = hop.at(i, b)
                    pe.wait_ge(h_out, n + 1)
                    after(pe, f_o, 2 * i + b - 1)
                    for k in range(nt):
                        last = nc.tensor.transpose(PF[b][:, k * P:(k + 1) * P], TH[b][:, k, :], ident[:, :])
                    last.then_inc(f_turn, 1)
                for b, nt in enumerate(SUB):
                    pe.wait_ge(f_tt, 2 * i + b + 1)
                    for k in range(nt):
                        last = nc.tensor.matmul(PF[b][:, k * P:(k + 1) * P], TT[b][:, k * P:(k + 1) * P], w32[:, :], start=True, stop=True)
                    last.then_inc(f_prod, 1)
            peeled(pe, IT, it)

        @block.scalar
        def _(act):
            def it(i):
                for b, nt in enumerate(SUB):
                    n, use, t, nt = hop.at(i, b)
                    act.wait_ge(h_z, n + 1)
                    after(act, f_turn, 2 * i + b - 1)
                    nc.scalar.activation(TH[b][:, 0:nt, :], Z[b][:, 0:nt, :], AF.Tanh).then_inc(h_out, 1)
                for b, nt in enumerate(SUB):
                    act.wait_ge(f_turn, 2 * i + b + 1)
                    after(act, f_prod, 2 * i + b - 1)
                    nc.scalar.activation(TT[b][:, 0:nt * P], PF[b][:, 0:nt * P], AF.Copy).then_inc(f_tt, 1)
            peeled(act, IT, it)
    end(ctx)
    top.close()


class _Rows:

    def __init__(self, array, tile):
        self.array, self.tile = array, tile

    def __getitem__(self, at):
        parts, j, cols = at
        return self.array[parts, bass.ds(self.tile + j, 1), cols].rearrange("p o d -> p (o d)")


_INS = ["x", "src", "dst", "edge_attr_128", "edge_weight", "L0_gnn_W1", "L0_gnn_b1", "L0_gnn_W2", "L0_gnn_b2", "L0_gnn_W3",
        "L0_gnn_b3", "L0_gnn_Wl", "L0_gnn_bl", "L1_gnn_eps", "L1_gnn_W1", "L1_gnn_b1", "L1_gnn_gamma1", "L1_gnn_beta1",
        "L1_gnn_W2", "L1_gnn_b2", "L1_gnn_gamma2", "L1_gnn_beta2", "L2_gnn_W_h_weight", "L2_gnn_W_h_bias", "L3_gnn_W1",
        "L3_gnn_b1", "L3_gnn_W2", "L3_gnn_b2"]


def kernel(**inputs):
    import concourse.bacc as bacc
    from concourse.bass_utils import run_bass_kernel_spmd as run

    nc = bacc.Bacc("TRN2", target_bir_lowering=False, num_devices=1)
    arrays, args = {}, []
    for name in _INS:
        a = np.ascontiguousarray(inputs[name])
        arrays[f"in_{name}"] = a
        args.append(nc.dram_tensor(f"in_{name}", a.shape, mybir.dt.from_np(a.dtype), kind="ExternalInput").ap())
    args.append(nc.dram_tensor("out_rows", (N, D), F32, kind="ExternalOutput").ap())
    build(nc, *args)
    return run(nc, [arrays], core_ids=[0]).results[0]["out_rows"]
```
